# Optimizing a Trainium2 kernel written in Bass

```python
import numpy as np
import jax
import jax.numpy as jnp

def _softmax(x, axis=-1):
    return jax.nn.softmax(x, axis=axis)

def _gelu(x):
    return jax.nn.gelu(x, approximate=True)

def _silu(x):
    return jax.nn.silu(x)

def _sigmoid(x):
    return jax.nn.sigmoid(x)

def _layernorm(x, axis=-1, eps=1e-05):
    m = jnp.mean(x, axis=axis, keepdims=True)
    v = jnp.var(x, axis=axis, keepdims=True)
    return (x - m) / jnp.sqrt(v + eps)

def _scatter_add(tgt, idx, src, axis=0):
    return tgt.at[idx].add(src)

def _segment_sum(src, seg, n):
    return jax.ops.segment_sum(src, seg, n)
kernel_name = 'mk_prb_d1_jaxref_r8_7ed714'

def setup_inputs(seed: int=0):
    np.random.seed(seed)
    _w = jnp.asarray

    def _L0_attn_setup():
        import jax, jax.numpy as jnp
        import numpy as np
        DIM = 128
        KV_DIM = 128
        WINDOW_SIZE = 64
        B, S = (2, 256)

        def _sliding_window_attention(m, q_w, q_b, k_w, k_b, v_w, v_b, window_size):
            Bsz, Seq, D = m.shape
            q = m @ q_w + q_b
            k = m @ k_w + k_b
            v = m @ v_w + v_b
            half = window_size // 2
            offsets = jnp.arange(-half, half + 1)
            idx = jnp.arange(Seq)[:, None] + offsets[None, :]
            valid = (idx >= 0) & (idx < Seq)
            idx_c = jnp.clip(idx, 0, Seq - 1)
            k_band = k[:, idx_c]
            v_band = v[:, idx_c]
            scale = 1.0 / jnp.sqrt(jnp.float32(D))
            scores = jnp.einsum('bsd,bswd->bsw', q, k_band) * scale
            scores = jnp.where(valid[None, :, :], scores, -jnp.inf)
            weights = jax.nn.softmax(scores, axis=-1)
            return jnp.einsum('bsw,bswd->bsd', weights, v_band)
        key = jax.random.key(seed)
        ks = jax.random.split(key, 12)
        w_scale = 1.0 / np.sqrt(DIM)
        return {'x': jax.random.normal(ks[0], (B, S, DIM), dtype=jnp.float32), 'nm_w1': jax.random.normal(ks[1], (DIM, KV_DIM), dtype=jnp.float32) * w_scale, 'nm_b1': jnp.zeros((KV_DIM,), dtype=jnp.float32), 'nm_w2': jax.random.normal(ks[2], (KV_DIM, DIM), dtype=jnp.float32) * w_scale, 'nm_b2': jnp.zeros((DIM,), dtype=jnp.float32), 'q_w': jax.random.normal(ks[3], (DIM, DIM), dtype=jnp.float32) * w_scale, 'q_b': jnp.zeros((DIM,), dtype=jnp.float32), 'k_w': jax.random.normal(ks[4], (DIM, DIM), dtype=jnp.float32) * w_scale, 'k_b': jnp.zeros((DIM,), dtype=jnp.float32), 'v_w': jax.random.normal(ks[5], (DIM, DIM), dtype=jnp.float32) * w_scale, 'v_b': jnp.zeros((DIM,), dtype=jnp.float32)}
    _L0_attn_in = _L0_attn_setup()

    def _L0_ffn_setup():
        import jax, jax.numpy as jnp
        import numpy as np
        B, S, H, F, E, K = (4, 512, 128, 512, 8, 2)
        LN_EPS = 1e-05
        key = jax.random.key(seed)
        kx, kr, k1, k2 = jax.random.split(key, 4)
        x = jax.random.normal(kx, (B, S, H), dtype=jnp.float32)
        gamma = jnp.ones((H,), jnp.float32)
        beta = jnp.zeros((H,), jnp.float32)
        Wr = jax.random.normal(kr, (H, E), jnp.float32) * 0.02
        br = jnp.zeros((E,), jnp.float32)
        W1 = jax.random.normal(k1, (E, H, F), jnp.float32) * (1.0 / np.sqrt(H))
        b1 = jnp.zeros((E, F), jnp.float32)
        W2 = jax.random.normal(k2, (E, F, H), jnp.float32) * (1.0 / np.sqrt(F))
        b2 = jnp.zeros((E, H), jnp.float32)
        return {'x': x, 'gamma': gamma, 'beta': beta, 'Wr': Wr, 'br': br, 'W1': W1, 'b1': b1, 'W2': W2, 'b2': b2}
    _L0_ffn_in = _L0_ffn_setup()
    _d = {'L0_attn_x': _L0_attn_in['x'], 'L0_attn_nm_w1': _L0_attn_in['nm_w1'], 'L0_attn_nm_b1': _L0_attn_in['nm_b1'], 'L0_attn_nm_w2': _L0_attn_in['nm_w2'], 'L0_attn_nm_b2': _L0_attn_in['nm_b2'], 'L0_attn_q_w': _L0_attn_in['q_w'], 'L0_attn_q_b': _L0_attn_in['q_b'], 'L0_attn_k_w': _L0_attn_in['k_w'], 'L0_attn_k_b': _L0_attn_in['k_b'], 'L0_attn_v_w': _L0_attn_in['v_w'], 'L0_attn_v_b': _L0_attn_in['v_b'], 'L0_ffn_gamma': _L0_ffn_in['gamma'], 'L0_ffn_beta': _L0_ffn_in['beta'], 'L0_ffn_Wr': _L0_ffn_in['Wr'], 'L0_ffn_br': _L0_ffn_in['br'], 'L0_ffn_W1': _L0_ffn_in['W1'], 'L0_ffn_b1': _L0_ffn_in['b1'], 'L0_ffn_W2': _L0_ffn_in['W2'], 'L0_ffn_b2': _L0_ffn_in['b2']}
    _x0 = _d['L0_attn_x']
    _d['L0_attn_x'] = jax.random.normal(jax.random.fold_in(jax.random.key(seed), 1), (4, 512, 128), dtype=_x0.dtype)
    del _x0
    return _d

def reference(L0_attn_x, L0_attn_nm_w1, L0_attn_nm_b1, L0_attn_nm_w2, L0_attn_nm_b2, L0_attn_q_w, L0_attn_q_b, L0_attn_k_w, L0_attn_k_b, L0_attn_v_w, L0_attn_v_b, L0_ffn_gamma, L0_ffn_beta, L0_ffn_Wr, L0_ffn_br, L0_ffn_W1, L0_ffn_b1, L0_ffn_W2, L0_ffn_b2):

    def _L0_attn_ref(x, nm_w1, nm_b1, nm_w2, nm_b2, q_w, q_b, k_w, k_b, v_w, v_b):
        import jax, jax.numpy as jnp
        import numpy as np
        DIM = 128
        KV_DIM = 128
        WINDOW_SIZE = 64
        B, S = (2, 256)

        def _sliding_window_attention(m, q_w, q_b, k_w, k_b, v_w, v_b, window_size):
            Bsz, Seq, D = m.shape
            q = m @ q_w + q_b
            k = m @ k_w + k_b
            v = m @ v_w + v_b
            half = window_size // 2
            offsets = jnp.arange(-half, half + 1)
            idx = jnp.arange(Seq)[:, None] + offsets[None, :]
            valid = (idx >= 0) & (idx < Seq)
            idx_c = jnp.clip(idx, 0, Seq - 1)
            k_band = k[:, idx_c]
            v_band = v[:, idx_c]
            scale = 1.0 / jnp.sqrt(jnp.float32(D))
            scores = jnp.einsum('bsd,bswd->bsw', q, k_band) * scale
            scores = jnp.where(valid[None, :, :], scores, -jnp.inf)
            weights = jax.nn.softmax(scores, axis=-1)
            return jnp.einsum('bsw,bswd->bsd', weights, v_band)
        h = jax.nn.relu(x @ nm_w1 + nm_b1)
        m = h @ nm_w2 + nm_b2
        return _sliding_window_attention(m, q_w, q_b, k_w, k_b, v_w, v_b, WINDOW_SIZE)

    def _L0_ffn_ref(x, gamma, beta, Wr, br, W1, b1, W2, b2):
        import jax, jax.numpy as jnp
        import numpy as np
        B, S, H, F, E, K = (4, 512, 128, 512, 8, 2)
        LN_EPS = 1e-05
        residual = x
        mu = jnp.mean(x, axis=-1, keepdims=True)
        var = jnp.var(x, axis=-1, keepdims=True)
        xn = (x - mu) * jax.lax.rsqrt(var + LN_EPS) * gamma + beta
        probs = jax.nn.softmax(xn @ Wr + br, axis=-1)
        scores, idx = jax.lax.top_k(probs, K)

        def expert_fn(w):
            W1_e, b1_e, W2_e, b2_e = w
            return jax.nn.relu(xn @ W1_e + b1_e) @ W2_e + b2_e
        full = jax.lax.map(expert_fn, (W1, b1, W2, b2))
        full = jnp.moveaxis(full, 0, 2)
        c = jnp.einsum('ef,efh->eh', jax.nn.relu(b1), W2) + b2
        c_total = c.sum(axis=0)
        sel_full = jnp.take_along_axis(full, idx[..., None], axis=2)
        c_sel = c[idx]
        output = jnp.sum(scores[..., None] * (sel_full - c_sel + c_total), axis=2)
        return residual + output
    x = L0_attn_x
    xn = _layernorm(x, axis=-1)
    x = x + _L0_attn_ref(xn, L0_attn_nm_w1, L0_attn_nm_b1, L0_attn_nm_w2, L0_attn_nm_b2, L0_attn_q_w, L0_attn_q_b, L0_attn_k_w, L0_attn_k_b, L0_attn_v_w, L0_attn_v_b) + _L0_ffn_ref(xn, L0_ffn_gamma, L0_ffn_beta, L0_ffn_Wr, L0_ffn_br, L0_ffn_W1, L0_ffn_b1, L0_ffn_W2, L0_ffn_b2)
    return x

_drawn_inputs = setup_inputs


def setup_inputs(seed=0):
    import zlib

    import numpy as np

    out = dict(_drawn_inputs(seed))
    spreads = {'L0_attn_nm_b1': (0.0, 0.406),
     'L0_attn_nm_b2': (0.0, 0.1),
     'L0_attn_q_b': (0.0, 0.8),
     'L0_attn_k_b': (0.0, 2.0),
     'L0_attn_v_b': (0.0, 0.1),
     'L0_ffn_gamma': (1.0, 0.2),
     'L0_ffn_beta': (0.0, 0.27),
     'L0_ffn_br': (0.0, 0.1),
     'L0_ffn_b1': (0.0, 0.273),
     'L0_ffn_b2': (0.0, 0.1)}
    factors = {'L0_attn_k_w': 2.724}
    for name, (base, spread) in spreads.items():
        noise = np.random.default_rng([zlib.crc32(name.encode()), seed]).standard_normal(out[name].shape)
        drawn = base * np.exp(spread * noise) if base else spread * noise
        out[name] = jnp.asarray(drawn.astype(out[name].dtype))
    for name, factor in factors.items():
        out[name] = (out[name] * factor).astype(out[name].dtype)
    return out
```

```python
import concourse.bass as bass
from concourse import mybir
from contextlib import ExitStack


def build(nc, x, nm_w1, nm_b1, nm_w2, nm_b2, q_w, q_b, k_w, k_b, v_w, v_b,
          gamma, beta, Wr, br, W1, b1, W2, b2, out):
    f32 = mybir.dt.float32
    i32 = mybir.dt.int32
    u32 = mybir.dt.uint32
    bf16 = mybir.dt.bfloat16
    ALU = mybir.AluOpType
    ACT = mybir.ActivationFunctionType
    AX = mybir.AxisListType.X

    P = 128
    B, S, H = x.shape
    E, _, F = W1.shape
    K = 2
    N = B * S
    TB = S // P
    NT = N // P
    FC = F // P
    HALF = 32
    WIN = P + 2 * HALF
    CH = WIN - P
    PADK = (TB + 1) * P
    EPS = 1e-5
    SCALE = float(H) ** -0.5
    NEG = -1e30
    ROW = H + 2
    GATE, DEST = H, H + 1
    REG = N + P
    MAXBLK = (N * K - E) // P + E
    NOWHERE = 1 << 20
    U = 3
    IT = MAXBLK // U
    assert H == P and TB == 4 and MAXBLK == U * IT and N * K // P >= E

    xt = x.rearrange("b (t p) h -> p (b t) h", p=P)
    ot = out.rearrange("b (t p) h -> p (b t) h", p=P)
    disp = nc.dram_tensor("disp", [E * REG + P, ROW], f32, kind="Internal").ap()
    ysel = nc.dram_tensor("ysel", [K * N, H], f32, kind="Internal").ap()
    yt = ysel.rearrange("(k t p) h -> p k t h", k=K, p=P)

    ctx = ExitStack()
    with ctx:
        def sb(name, shape, dt=f32):
            return ctx.enter_context(nc.sbuf_tensor(name, shape, dt))

        def sem(name):
            return ctx.enter_context(nc.semaphore(name))

        ident = sb("ident", [P, P])
        upper = sb("upper", [P, P], bf16)
        ones = sb("ones", [P, P], bf16)
        minus_half = sb("minus_half", [P, TB])
        band = sb("band", [P, TB, WIN])
        iota_e = sb("iota_e", [P, E])
        region = sb("region", [P, E])
        iota_j = sb("iota_j", [1, MAXBLK])
        iota_128 = sb("iota_128", [1, NT])
        one_row = sb("one_row", [1, E])
        padrow = sb("padrow", [P, ROW])
        w1_sb = sb("w1_sb", [H, H])
        w2_sb = sb("w2_sb", [H, H])
        wq_sb = sb("wq_sb", [H, H])
        wk_sb = sb("wk_sb", [H, H])
        wv_sb = sb("wv_sb", [H, H])
        wr_sb = sb("wr_sb", [H, E])
        br_bc = sb("br_bc", [P, E])
        vb_bc = sb("vb_bc", [P, H])
        NROWS = E * FC + E + 6
        B2, NB1, NB2, QB, KB, GA, BE = E * FC, E * FC + E, NROWS - 5, NROWS - 4, NROWS - 3, NROWS - 2, NROWS - 1
        rows = sb("rows", [NROWS, H])
        cols = sb("cols", [P, NROWS])
        qbs = sb("qbs", [P, 1])
        W1x = sb("W1x", [H, E, F + FC])
        W2s = sb("W2s", [P, E, FC, H])
        x_sb = sb("x_sb", [P, NT, H])
        xn = sb("xn", [P, NT, H])
        stats = sb("stats", [P, 2, NT, 6])
        mv = sb("mv", [P, 2, NT, 2])
        veps = sb("veps", [P, 2, NT])
        rstd = sb("rstd", [P, 2, NT])
        zrow = sb("zrow", [P, NT, K, ROW])
        lg = sb("lg", [P, NT, E])
        best = sb("best", [P, NT, 8])
        bidx = sb("bidx", [P, NT, 8], u32)
        bidxf = sb("bidxf", [P, NT, K])
        rel = sb("rel", [P, NT, E])
        erel = sb("erel", [P, NT, E])
        esum = sb("esum", [P, NT])
        einv = sb("einv", [P, NT])
        gates = sb("gates", [P, NT, K])
        oh = sb("oh", [P, NT, K, E])
        mask = sb("mask", [P, NT, E], bf16)
        msum = sb("msum", [P, B, E], bf16)
        before = sb("before", [P, B + 1, E], bf16)
        slot = sb("slot", [P, NT, E])
        ohslot = sb("ohslot", [P, NT, K, E])
        pos = sb("pos", [P, NT, K], i32)
        ohg = sb("ohg", [P, NT, K, E])
        gfull = sb("gfull", [P, NT, E])
        over = sb("over", [1, E, NT])
        nblk = sb("nblk", [1, E])
        count_i = sb("count_i", [1, E], i32)
        incl = sb("incl", [1, E])
        past = sb("past", [1, MAXBLK, E])
        pastn = sb("pastn", [1, MAXBLK, E])
        eb = sb("eb", [1, MAXBLK])
        excl = sb("excl", [1, MAXBLK])
        jrel = sb("jrel", [1, MAXBLK])
        startf = sb("startf", [1, MAXBLK])
        start_i = sb("start_i", [1, MAXBLK], i32)
        expert_i = sb("expert_i", [1, MAXBLK], i32)
        xnT = sb("xnT", [H, 2, S])
        xn2T = sb("xn2T", [H, 2, S])
        h1T = sb("h1T", [H, S])
        mT = sb("mT", [H, 2, PADK])
        qT = sb("qT", [H, B, S])
        kT = sb("kT", [H, B, PADK])
        v = sb("v", [P, B, TB + 1, H])
        sm = sb("sm", [P, 2, TB, WIN])
        nmax = sb("nmax", [P, 2, TB])
        prob = sb("prob", [P, 2, TB, WIN])
        psums = sb("psums", [P, 2, TB])
        pinv = sb("pinv", [P, 2, TB])
        pTa = sb("pTa", [P, TB, P])
        pTb = sb("pTb", [CH, TB, P])
        gT = sb("gT", [E, TB, P])
        acc = sb("acc", [P, NT, H])
        rb1 = sb("rb1", [P, E * FC])
        c_e = sb("c_e", [H, E])
        c_tot = sb("c_tot", [H, 1])
        bc = sb("bc", [H, E])
        dT = sb("dT", [H, E])
        d_rows = sb("d_rows", [E, H])
        xg = sb("xg", [P, U, ROW])
        meta_g = sb("meta_g", [P, U])
        meta_d = sb("meta_d", [P, MAXBLK], i32)
        xgT = sb("xgT", [H, U, P])
        w1c = sb("w1c", [H, U, F + FC])
        hT = sb("hT", [P, U, FC, P])
        ys = sb("ys", [P, U, H])
        yk = sb("yk", [P, K, NT, H])

        bank = [ctx.enter_context(nc.psum_tensor(f"bank{i}", [P, 512], f32)) for i in range(8)]

        def tiles(i):
            return bank[i][:, :].rearrange("p (t c) -> p t c", t=TB)

        xT_ps, zT_ps = tiles(0), tiles(1)
        s_ps = [bank[i][:, :].rearrange("p (t c) -> p t c", t=2) for i in (0, 1)]
        pTa_ps, pTb_ps = tiles(2), tiles(3)
        logit_ps = bank[4][:, 0:NT * E].rearrange("p (t e) -> p t e", e=E)
        rank_ps = bank[4][:, NT * E:2 * NT * E].rearrange("p (t e) -> p t e", e=E)
        small_ps = bank[7]
        total_ps = bank[4][:, 2 * NT * E:2 * NT * E + E]
        cols_ps = small_ps[:, 0:NROWS]
        c_ps = small_ps[:, 136:136 + E]
        d_ps = small_ps[0:E, 256:256 + H]
        gT_ps = bank[4][0:E, :].rearrange("p (t c) -> p t c", t=TB)
        pv_ps, gd_ps = tiles(5), tiles(6)
        h_ps = [[bank[i][:, 0:F // 2].rearrange("p (c t) -> p c t", t=P) for i in pair] for pair in ((0, 1), (2, 4), (5, 6))]
        xgT_ps = tiles(3)
        y_ps = tiles(7)

        x_in = [sem(f"x_in{b}") for b in range(B)]
        rows_in = sem("rows_in")
        wr_in = sem("wr_in")
        wa_in = sem("wa_in")
        wv_in = sem("wv_in")
        vb_in = sem("vb_in")
        W1_in = sem("W1_in")
        W2_in = sem("W2_in")
        pads_out = sem("pads_out")
        sent = sem("sent")
        xg_in = [sem(f"xg_in{s}") for s in range(U)]
        y_out = [sem(f"y_out{s}") for s in range(U)]
        yk_in = [sem(f"yk_in{b}") for b in range(B)]
        stored = sem("stored")
        (consts, ident_ok, cols_t, cols_ok, stat1, var1, rstd1, xn_ok, stat2, var2, rstd2, z_ok,
         xz_t, xnT_ok, xn2T_ok, logit_t, lg_ok, best_ok, rel_ok, erel_ok, esum_ok, einv_ok, gate_ok,
         idx_ok, idxf_ok, oh_ok, mask_ok, msum_ok, before_ok, rank_t, slot_ok, ohslot_ok, pos_ok,
         ohg_ok, gfull_ok, h1_t, h1_ok, m_t, m_ok, k_t, k_ok, q_t, q_ok, v_t, v_ok,
         total_t, table, table_ok, s_t, sm_ok, nmax_ok, prob_ok, pT_t, pTa_ok, pTb_ok, pinv_ok,
         pv_t, attn_ok, gT_t, gT_ok, gd_t, acc_ok, base_ok, c_t, cstep, d_ready, dT_t, d_ok,
         xgT_t, xgT_ok, meta_ok, w1c_ok, h_t0, h_t1, h_act_ok, h_dve_ok, y_t, y_ok, sum_ok, out_ok,
         const_step, free_zero, pw1, pw2) = [sem(n) for n in (
             "consts ident_ok cols_t cols_ok stat1 var1 rstd1 xn_ok stat2 var2 rstd2 z_ok "
             "xz_t xnT_ok xn2T_ok logit_t lg_ok best_ok rel_ok erel_ok esum_ok einv_ok gate_ok "
             "idx_ok idxf_ok oh_ok mask_ok msum_ok before_ok rank_t slot_ok ohslot_ok pos_ok "
             "ohg_ok gfull_ok h1_t h1_ok m_t m_ok k_t k_ok q_t q_ok v_t v_ok "
             "total_t table table_ok s_t sm_ok nmax_ok prob_ok pT_t pTa_ok pTb_ok pinv_ok "
             "pv_t attn_ok gT_t gT_ok gd_t acc_ok base_ok c_t cstep d_ready dT_t d_ok "
             "xgT_t xgT_ok meta_ok w1c_ok h_t0 h_t1 h_act_ok h_dve_ok y_t y_ok sum_ok out_ok "
             "const_step free_zero pw1 pw2").split()]

        block = ctx.enter_context(nc.Block())

        @block.sync
        def _(sp):
            for b in range(B):
                sp.dma_start(x_sb[:, TB * b:TB * b + TB, :], xt[:, TB * b:TB * b + TB, :]).then_inc(x_in[b], 16)
            sp.dma_start(W1x[:, :, 0:F], W1.rearrange("e h f -> h e f")).then_inc(W1_in, 16)
            sp.dma_start(W2s[:, :, :, :], W2.rearrange("e (c p) h -> p e c h", p=P)).then_inc(W2_in, 16)
            sp.wait_ge(consts, 1)
            sp.dma_start(disp[E * REG:E * REG + P, :], padrow[:, :]).then_inc(pads_out, 16)
            sp.wait_ge(table_ok, 1)
            for e in range(E):
                n = sp.value_load(count_i[0:1, e:e + 1], min_val=0, max_val=N)
                sp.dma_start(disp[bass.ds(n + e * REG, P), :], padrow[:, :]).then_inc(pads_out, 16)
            sp.wait_ge(pads_out, 16 * (E + 1))
            sp.wait_ge(sent, 16 * NT * K)

            def load_block(j, s):
                r = sp.value_load(start_i[0:1, bass.ds(j, 1)], min_val=0, max_val=E * REG)
                sp.dma_start(xg[:, s, :], disp[bass.ds(r, P), :]).then_inc(xg_in[s], 16)

            for s in range(U):
                load_block(s, s)
            with sp.Fori(1, IT) as it:
                for s in range(U):
                    sp.wait_ge(xgT_t, U * it - U + s + 1)
                    sp.wait_ge(meta_ok, U * it - U + s + 1)
                    load_block(U * it + s, s)

            for s in range(U):
                sp.wait_ge(y_out[s], 16 * IT)
            for b in range(0, B, 2):
                sp.dma_start(yk[:, 0, TB * b:TB * b + TB, :], yt[:, 0, TB * b:TB * b + TB, :]).then_inc(yk_in[b], 16)
                sp.dma_start(yk[:, 1, TB * b:TB * b + TB, :], yt[:, 1, TB * b:TB * b + TB, :]).then_inc(yk_in[b], 16)
            for b in range(B):
                sp.wait_ge(out_ok, b + 1)
                sp.dma_start(ot[:, TB * b:TB * b + TB, :], acc[:, TB * b:TB * b + TB, :]).then_inc(stored, 16)
            sp.wait_ge(stored, 16 * B)

        @block.gpsimd
        def _(pool):
            g = nc.gpsimd
            g.memset(ident[:, :], 0.0)
            g.memset(upper[:, :], 0.0)
            g.memset(minus_half[:, :], -0.5)
            g.memset(band[:, :, :], 0.0)
            g.memset(padrow[:, :], 0.0).then_inc(const_step, 1)
            pool.wait_ge(const_step, 1)
            g.affine_select(out=ident[:, :], in_=ident[:, :], compare_op=ALU.not_equal, fill=1.0,
                            base=0, pattern=[[-1, P]], channel_multiplier=1).then_inc(ident_ok, 1)
            g.memset(padrow[:, DEST:DEST + 1], float(NOWHERE))
            g.affine_select(out=upper[:, :], in_=upper[:, :], compare_op=ALU.is_ge, fill=1.0,
                            base=0, pattern=[[-1, P]], channel_multiplier=1)
            g.affine_select(out=band[:, :, :], in_=band[:, :, :], compare_op=ALU.is_ge, fill=NEG,
                            base=0, pattern=[[0, TB], [1, WIN]], channel_multiplier=-1).then_inc(const_step, 1)
            pool.wait_ge(const_step, 2)
            g.affine_select(out=band[:, :, :], in_=band[:, :, :], compare_op=ALU.is_ge, fill=NEG,
                            base=2 * HALF, pattern=[[0, TB], [-1, WIN]], channel_multiplier=1).then_inc(const_step, 1)
            pool.wait_ge(const_step, 3)
            g.memset(band[:, 0, 0:HALF], NEG)
            g.memset(band[:, TB - 1, HALF + P:WIN], NEG)
            g.iota(iota_e[:, :], pattern=[[1, E]], base=0, channel_multiplier=0,
                   allow_small_or_imprecise_dtypes=True)
            g.iota(region[:, :], pattern=[[REG, E]], base=0, channel_multiplier=0,
                   allow_small_or_imprecise_dtypes=True)
            g.iota(iota_j[:, :], pattern=[[1, MAXBLK]], base=0, channel_multiplier=0,
                   allow_small_or_imprecise_dtypes=True)
            g.iota(iota_128[:, :], pattern=[[P, NT]], base=0, channel_multiplier=0,
                   allow_small_or_imprecise_dtypes=True)
            g.iota(zrow[:, :, :, DEST:DEST + 1].rearrange("p t k o -> p t (k o)"),
                   pattern=[[P, NT], [N, K]], base=0, channel_multiplier=1,
                   allow_small_or_imprecise_dtypes=True).then_inc(consts, 1)

            def inverse_root(l, b, var, done):
                pool.wait_ge(var, b + 1)
                g.tensor_tensor(rstd[:, l, TB * b:TB * b + TB], veps[:, l, TB * b:TB * b + TB],
                                minus_half[:, :], ALU.pow).then_inc(done, 1)

            def send(b, k):
                for t in range(TB * b, TB * b + TB):
                    g.indirect_dma_start(disp[:, :], bass.IndirectOffsetOnAxis(ap=pos[:, t, k:k + 1], axis=0),
                                         zrow[:, t, k, :], None).then_inc(sent, 16)

            for b in range(2):
                inverse_root(0, b, var1, rstd1)
                inverse_root(1, b, var2, rstd2)
            for b in range(B):
                if b + 2 < B:
                    inverse_root(0, b + 2, var1, rstd1)
                pool.wait_ge(pos_ok, b + 1)
                pool.wait_ge(gate_ok, b + 1)
                send(b, 0)
                if b + 2 < B:
                    inverse_root(1, b + 2, var2, rstd2)
                send(b, 1)

            def take_meta(j, s, value):
                pool.wait_ge(xg_in[s], value)
                g.tensor_copy(meta_g[:, s:s + 1], xg[:, s, GATE:GATE + 1])
                g.tensor_copy(meta_d[:, j:j + 1], xg[:, s, DEST:DEST + 1]).then_inc(meta_ok, 1)

            def send_back(j, s):
                pool.wait_ge(y_ok, j + 1)
                g.indirect_dma_start(ysel[:, :], bass.IndirectOffsetOnAxis(ap=meta_d[:, j:j + 1], axis=0),
                                     ys[:, s, :], None, bounds_check=K * N - 1, oob_is_err=False).then_inc(y_out[s], 16)

            pool.wait_ge(vb_in, 16)
            for b in range(B):
                a = acc[:, TB * b:TB * b + TB, :]
                pool.wait_ge(acc_ok, b + 1)
                g.tensor_tensor(a, a, x_sb[:, TB * b:TB * b + TB, :], ALU.add).then_inc(base_ok, 1)
                pool.wait_ge(base_ok, 2 * b + 1)
                g.tensor_tensor(a, a, vb_bc[:, :].unsqueeze(1).to_broadcast([P, TB, H]), ALU.add).then_inc(base_ok, 1)
            for s in range(U):
                take_meta(s, s, 16)
            for j in range(MAXBLK):
                send_back(j, j % U)
                if j + U < MAXBLK:
                    take_meta(j + U, j % U, 16 * (j // U) + 32)

        @block.vector
        def _(dve):
            v_ = nc.vector

            def per_tile(ap, width):
                return ap.unsqueeze(2).to_broadcast([P, TB, width])

            def norm1_stats(b):
                dve.wait_ge(x_in[b], 16)
                for t in range(TB * b, TB * b + TB):
                    last = v_.bn_stats(stats[:, 0, t, :], x_sb[:, t, :])
                last.then_inc(stat1, 1)
                dve.wait_ge(stat1, 2 * b + 1)
                for t in range(TB * b, TB * b + TB):
                    last = v_.bn_aggr(mv[:, 0, t, :], stats[:, 0, t, :])
                last.then_inc(stat1, 1)
                dve.wait_ge(stat1, 2 * b + 2)
                v_.tensor_scalar(veps[:, 0, TB * b:TB * b + TB], mv[:, 0, TB * b:TB * b + TB, 1], EPS, None,
                                 ALU.add).then_inc(var1, 1)

            def norm1_apply(b):
                dve.wait_ge(rstd1, b + 1)
                for t in range(TB * b, TB * b + TB):
                    last = v_.tensor_scalar(xn[:, t, :], x_sb[:, t, :], mv[:, 0, t, 0:1], rstd[:, 0, t:t + 1],
                                            ALU.subtract, ALU.mult)
                last.then_inc(xn_ok, 1)
                dve.wait_ge(xn_ok, b + 1)
                for t in range(TB * b, TB * b + TB):
                    last = v_.bn_stats(stats[:, 1, t, :], xn[:, t, :])
                last.then_inc(stat2, 1)
                dve.wait_ge(stat2, 2 * b + 1)
                for t in range(TB * b, TB * b + TB):
                    last = v_.bn_aggr(mv[:, 1, t, :], stats[:, 1, t, :])
                last.then_inc(stat2, 1)
                dve.wait_ge(stat2, 2 * b + 2)
                v_.tensor_scalar(veps[:, 1, TB * b:TB * b + TB], mv[:, 1, TB * b:TB * b + TB, 1], EPS, None,
                                 ALU.add).then_inc(var2, 1)

            def norm2_apply(b):
                dve.wait_ge(rstd2, b + 1)
                for t in range(TB * b, TB * b + TB):
                    last = v_.tensor_scalar(zrow[:, t, :, 0:H], xn[:, t, :].unsqueeze(1).to_broadcast([P, K, H]),
                                            mv[:, 1, t, 0:1], rstd[:, 1, t:t + 1], ALU.subtract, ALU.mult)
                last.then_inc(z_ok, 1)

            def choose(b):
                ts = slice(TB * b, TB * b + TB)
                dve.wait_ge(logit_t, b + 1)
                v_.tensor_tensor(lg[:, ts, :], logit_ps[:, ts, :], br_bc[:, :].unsqueeze(1).to_broadcast([P, TB, E]),
                                 ALU.add).then_inc(lg_ok, 1)
                dve.wait_ge(lg_ok, b + 1)
                for t in range(TB * b, TB * b + TB):
                    last = v_.max(best[:, t, :], lg[:, t, :])
                last.then_inc(best_ok, 1)
                dve.wait_ge(best_ok, b + 1)
                v_.tensor_tensor(rel[:, ts, :], best[:, ts, :], best[:, ts, 0:1].to_broadcast([P, TB, E]),
                                 ALU.subtract).then_inc(rel_ok, 1)
                for t in range(TB * b, TB * b + TB):
                    last = v_.max_index(bidx[:, t, :], best[:, t, :], lg[:, t, :])
                last.then_inc(idx_ok, 1)
                dve.wait_ge(idx_ok, b + 1)
                v_.tensor_copy(bidxf[:, ts, :], bidx[:, ts, 0:K]).then_inc(idxf_ok, 1)
                dve.wait_ge(idxf_ok, b + 1)
                v_.tensor_tensor(oh[:, ts, :, :].rearrange("p t k e -> p (t k) e"),
                                 iota_e[:, :].unsqueeze(1).to_broadcast([P, TB * K, E]),
                                 bidxf[:, ts, :].rearrange("p t k -> p (t k)").unsqueeze(2).to_broadcast([P, TB * K, E]),
                                 ALU.is_equal).then_inc(oh_ok, 1)
                dve.wait_ge(oh_ok, b + 1)
                v_.tensor_tensor(mask[:, ts, :], oh[:, ts, 0, :], oh[:, ts, 1, :], ALU.add).then_inc(mask_ok, 1)
                dve.wait_ge(erel_ok, b + 1)
                v_.tensor_reduce(esum[:, ts], erel[:, ts, :], AX, ALU.add).then_inc(esum_ok, 1)
                dve.wait_ge(mask_ok, b + 1)
                with nc.allow_low_precision("counts up to 16 are exact in bfloat16"):
                    v_.tensor_reduce(msum[:, b, :], mask[:, ts, :].rearrange("p t e -> p e t"), AX,
                                     ALU.add).then_inc(msum_ok, 1)
                dve.wait_ge(esum_ok, b + 1)
                v_.reciprocal(einv[:, ts], esum[:, ts]).then_inc(einv_ok, 1)
                dve.wait_ge(msum_ok, b + 1)
                v_.tensor_tensor(before[:, b + 1, :], before[:, b, :], msum[:, b, :], ALU.add).then_inc(before_ok, 1)
                dve.wait_ge(einv_ok, b + 1)
                v_.tensor_tensor(zrow[:, ts, :, GATE], erel[:, ts, 0:K],
                                 einv[:, ts].unsqueeze(2).to_broadcast([P, TB, K]), ALU.mult).then_inc(gate_ok, 1)

            def place(b):
                ts = slice(TB * b, TB * b + TB)
                dve.wait_ge(rank_t, b + 1)
                v_.tensor_tensor(slot[:, ts, :], rank_ps[:, ts, :], region[:, :].unsqueeze(1).to_broadcast([P, TB, E]),
                                 ALU.add).then_inc(slot_ok, 1)
                dve.wait_ge(slot_ok, b + 1)
                v_.tensor_tensor(ohslot[:, ts, :, :], oh[:, ts, :, :],
                                 slot[:, ts, :].unsqueeze(2).to_broadcast([P, TB, K, E]), ALU.mult).then_inc(ohslot_ok, 1)
                dve.wait_ge(ohslot_ok, b + 1)
                with nc.allow_low_precision("whole numbers below 2 ** 24, summed in float32"):
                    v_.tensor_reduce(pos[:, ts, :].rearrange("p t k -> p (t k)"),
                                     ohslot[:, ts, :, :].rearrange("p t k e -> p (t k) e"), AX,
                                     ALU.add).then_inc(pos_ok, 1)
                dve.wait_ge(gate_ok, b + 1)
                v_.tensor_tensor(ohg[:, ts, :, :].rearrange("p t k e -> p (t k) e"),
                                 oh[:, ts, :, :].rearrange("p t k e -> p (t k) e"),
                                 zrow[:, ts, :, GATE:GATE + 1].rearrange("p t k o -> p (t k) o").to_broadcast([P, TB * K, E]),
                                 ALU.mult).then_inc(ohg_ok, 1)
                dve.wait_ge(ohg_ok, b + 1)
                v_.tensor_tensor(gfull[:, ts, :], ohg[:, ts, 0, :], ohg[:, ts, 1, :], ALU.add).then_inc(gfull_ok, 1)

            v_.memset(before[:, 0, :], 0.0)
            v_.memset(ones[:, :], 1.0)
            v_.memset(one_row[:, :], 1.0)
            v_.memset(mT[:, :, 0:HALF], 0.0)
            v_.memset(mT[:, :, HALF + S:PADK], 0.0)
            v_.memset(kT[:, :, 0:HALF], 0.0)
            v_.memset(kT[:, :, HALF + S:PADK], 0.0).then_inc(free_zero, 1)
            for b in range(2):
                norm1_stats(b)
                norm1_apply(b)
                norm2_apply(b)
            dve.wait_ge(consts, 1)
            dve.wait_ge(wr_in, 32)
            for b in range(B):
                choose(b)
                if b + 2 < B:
                    norm1_stats(b + 2)
                place(b)
                if b + 2 < B:
                    norm1_apply(b + 2)
                    norm2_apply(b + 2)

            steps = [0]

            def after(ins):
                steps[0] += 1
                ins.then_inc(table, 1)
                dve.wait_ge(table, steps[0])

            dve.wait_ge(total_t, 1)
            v_.tensor_copy(count_i[:, :], total_ps[0:1, :])
            after(v_.tensor_tensor(over[:, :, :], total_ps[0:1, :].unsqueeze(2).to_broadcast([1, E, NT]),
                                   iota_128[:, :].unsqueeze(1).to_broadcast([1, E, NT]), ALU.is_gt))
            after(v_.tensor_reduce(nblk[:, :], over[:, :, :], AX, ALU.add))
            after(v_.tensor_tensor_scan(incl[:, :], one_row[:, :], nblk[:, :], 0.0, ALU.mult, ALU.add))
            after(v_.tensor_tensor(past[:, :, :], iota_j[:, :].unsqueeze(2).to_broadcast([1, MAXBLK, E]),
                                   incl[:, :].unsqueeze(1).to_broadcast([1, MAXBLK, E]), ALU.is_ge))
            after(v_.tensor_tensor(pastn[:, :, :], past[:, :, :],
                                   nblk[:, :].unsqueeze(1).to_broadcast([1, MAXBLK, E]), ALU.mult))
            v_.tensor_reduce(eb[:, :], past[:, :, :], AX, ALU.add)
            after(v_.tensor_reduce(excl[:, :], pastn[:, :, :], AX, ALU.add))
            v_.tensor_scalar(expert_i[:, :], eb[:, :], float(E - 1), None, ALU.min)
            after(v_.tensor_tensor(jrel[:, :], iota_j[:, :], excl[:, :], ALU.subtract))
            after(v_.tensor_scalar(startf[:, :], eb[:, :], float(REG), None, ALU.mult))
            after(v_.scalar_tensor_tensor(startf[:, :], jrel[:, :], float(P), startf[:, :], ALU.mult, ALU.add))
            v_.tensor_scalar(start_i[:, :], startf[:, :], float(E * REG), None, ALU.min).then_inc(table_ok, 1)

            dve.wait_ge(c_t, 1)
            v_.tensor_tensor(c_e[:, :], c_ps, cols[:, B2:B2 + E], ALU.add).then_inc(cstep, 1)
            dve.wait_ge(cstep, 1)
            v_.tensor_reduce(c_tot[:, :], c_e[:, :], AX, ALU.add)
            v_.tensor_tensor(bc[:, :], cols[:, B2:B2 + E], c_e[:, :], ALU.subtract).then_inc(cstep, 1)
            dve.wait_ge(cstep, 2)
            v_.tensor_scalar(dT[:, :], bc[:, :], c_tot[:, 0:1], None, ALU.add).then_inc(d_ready, 1)

            def soften(b):
                for h in range(2):
                    dve.wait_ge(s_t, 2 * b + h + 1)
                    v_.tensor_tensor(sm[:, b % 2, 2 * h:2 * h + 2, :], s_ps[h][:, :, 0:WIN],
                                     band[:, 2 * h:2 * h + 2, :], ALU.add).then_inc(sm_ok, 1)
                    dve.wait_ge(sm_ok, 2 * b + h + 1)
                    v_.tensor_reduce(nmax[:, b % 2, 2 * h:2 * h + 2], sm[:, b % 2, 2 * h:2 * h + 2, :], AX, ALU.max,
                                     negate=True).then_inc(nmax_ok, 1)

            def attention_end(b):
                ts = slice(TB * b, TB * b + TB)
                dve.wait_ge(pT_t, b + 1)
                if b == 0:
                    dve.wait_ge(dT_t, 1)
                    v_.tensor_copy(d_rows[:, :], d_ps).then_inc(d_ok, 1)
                v_.tensor_copy(pTb[:, :, :], pTb_ps[0:CH, :, :]).then_inc(pTb_ok, 1)
                v_.reciprocal(pinv[:, b % 2, :], psums[:, b % 2, :]).then_inc(pinv_ok, 1)
                dve.wait_ge(pinv_ok, b + 1)
                dve.wait_ge(pv_t, b + 1)
                for i in range(TB):
                    t = TB * b + i
                    last = v_.scalar_tensor_tensor(acc[:, t, :], pv_ps[:, i, :], pinv[:, b % 2, i:i + 1], xn[:, t, :],
                                                   ALU.mult, ALU.add)
                last.then_inc(attn_ok, 1)
                dve.wait_ge(attn_ok, b + 1)
                v_.tensor_tensor(acc[:, ts, :], gd_ps, acc[:, ts, :], ALU.add).then_inc(acc_ok, 1)

            soften(0)
            for b in range(B):
                if b + 1 < B:
                    soften(b + 1)
                attention_end(b)

            def take_w1(j, s):
                e = dve.value_load(expert_i[0:1, bass.ds(j, 1)], min_val=0, max_val=E - 1)
                v_.tensor_copy(w1c[:, s, :], W1x[:, bass.ds(e, 1), :].rearrange("p o f -> p (o f)")).then_inc(w1c_ok, 1)

            def relu_half(j, s):
                dve.wait_ge(h_t1, j + 1)
                dve.wait_ge(w1c_ok, j + 1)
                for c in range(FC // 2, FC):
                    last = v_.tensor_scalar(hT[:, s, c, :], h_ps[s][1][:, c - FC // 2, :], w1c[:, s, F + c:F + c + 1], 0.0,
                                            ALU.add, ALU.max)
                last.then_inc(h_dve_ok, 1)

            def weigh(j, s, it):
                dve.wait_ge(y_t, j + 1)
                dve.wait_ge(meta_ok, j + 1)
                if it is not None:
                    dve.wait_ge(y_out[s], 16 * it)
                v_.tensor_scalar(ys[:, s, :], y_ps[:, s, :], meta_g[:, s:s + 1], None, ALU.mult).then_inc(y_ok, 1)

            dve.wait_ge(W1_in, 16)
            dve.wait_ge(cols_ok, 2)
            take_w1(0, 0)
            take_w1(1, 1)
            relu_half(0, 0)

            def expert_step(j, s, it, ahead2, ahead1):
                if ahead2:
                    take_w1(j + 2, (s + 2) % U)
                if ahead1:
                    relu_half(j + 1, (s + 1) % U)
                weigh(j, s, it)

            for s in range(U):
                expert_step(s, s, None, True, True)
            with dve.Fori(1, IT - 1) as it:
                for s in range(U):
                    expert_step(U * it + s, s, it, True, True)
            for s in range(U):
                expert_step(U * (IT - 1) + s, s, IT - 1, s + 2 < U, s + 1 < U)

            for b in range(B):
                ts = slice(TB * b, TB * b + TB)
                dve.wait_ge(yk_in[b], 32)
                dve.wait_ge(base_ok, 2 * b + 2)
                v_.tensor_tensor(acc[:, ts, :], acc[:, ts, :], yk[:, 0, ts, :], ALU.add).then_inc(sum_ok, 1)
                dve.wait_ge(sum_ok, b + 1)
                v_.tensor_tensor(acc[:, ts, :], acc[:, ts, :], yk[:, 1, ts, :], ALU.add).then_inc(out_ok, 1)

        @block.scalar
        def _(act):
            a_ = nc.scalar
            for i, src in enumerate((nm_b1, nm_b2, q_b, k_b, gamma, beta)):
                act.dma_start(rows[NB1 + i:NB1 + i + 1, :], src.unsqueeze(0)).then_inc(rows_in, 16)
            act.dma_start(rows[0:B2, :], b1.rearrange("e (c p) -> (e c) p", p=P)).then_inc(rows_in, 16)
            act.dma_start(rows[B2:B2 + E, :], b2).then_inc(rows_in, 16)
            act.dma_start(wr_sb[:, :], Wr).then_inc(wr_in, 16)
            act.dma_start(br_bc[:, :], br.partition_broadcast(P)).then_inc(wr_in, 16)
            act.dma_start(w1_sb[:, :], nm_w1).then_inc(wa_in, 16)
            act.dma_start(w2_sb[:, :], nm_w2).then_inc(wa_in, 16)
            act.dma_start(wk_sb[:, :], k_w).then_inc(wa_in, 16)
            act.dma_start(wq_sb[:, :], q_w).then_inc(wa_in, 16)
            act.dma_start(wv_sb[:, :], v_w).then_inc(wv_in, 16)
            act.dma_start(vb_bc[:, :], v_b.partition_broadcast(P)).then_inc(vb_in, 16)

            act.wait_ge(cols_t, 1)
            a_.activation(cols[:, :], cols_ps, ACT.Copy).then_inc(cols_ok, 1)
            act.wait_ge(cols_ok, 1)
            a_.activation(qbs[:, :], cols[:, QB:QB + 1], ACT.Copy, scale=SCALE)
            a_.activation(rb1[:, :], cols[:, 0:E * FC], ACT.Relu)
            act.wait_ge(W1_in, 16)
            a_.activation(W1x[:, :, F:F + FC], cols[:, 0:E * FC].rearrange("p (e c) -> p e c", c=FC),
                          ACT.Copy).then_inc(cols_ok, 1)

            def turned(b):
                act.wait_ge(xz_t, b + 1)
                a_.activation(xn2T[:, b % 2, :], zT_ps.rearrange("p t c -> p (t c)"), ACT.Identity,
                              bias=cols[:, BE:BE + 1], scale=cols[:, GA:GA + 1]).then_inc(xn2T_ok, 1)
                a_.activation(xnT[:, b % 2, :], xT_ps.rearrange("p t c -> p (t c)"), ACT.Copy).then_inc(xnT_ok, 1)

            act.wait_ge(cols_ok, 2)
            turned(0)
            act.wait_ge(free_zero, 1)
            for b in range(B):
                act.wait_ge(h1_t, b + 1)
                a_.activation(h1T[:, :], bank[2][:, :], ACT.Relu, bias=cols[:, NB1:NB1 + 1]).then_inc(h1_ok, 1)
                if b + 1 < B:
                    turned(b + 1)
                act.wait_ge(rel_ok, b + 1)
                a_.activation(erel[:, TB * b:TB * b + TB, :], rel[:, TB * b:TB * b + TB, :], ACT.Exp).then_inc(erel_ok, 1)
                act.wait_ge(m_t, b + 1)
                a_.activation(mT[:, b % 2, HALF:HALF + S], bank[3][:, :], ACT.Identity,
                              bias=cols[:, NB2:NB2 + 1]).then_inc(m_ok, 1)
                act.wait_ge(k_t, b + 1)
                a_.activation(kT[:, b, HALF:HALF + S], bank[2][:, :], ACT.Identity,
                              bias=cols[:, KB:KB + 1]).then_inc(k_ok, 1)
                act.wait_ge(q_t, b + 1)
                a_.activation(qT[:, b, :], bank[3][:, :], ACT.Identity, bias=qbs[:, 0:1], scale=SCALE).then_inc(q_ok, 1)
                act.wait_ge(v_t, b + 1)
                a_.activation(v[:, b, 0:TB, :], pv_ps, ACT.Copy)
                a_.activation(v[:, b, TB, :], gd_ps[:, 0, :], ACT.Copy).then_inc(v_ok, 1)

            def exps(b):
                for h in range(2):
                    act.wait_ge(nmax_ok, 2 * b + h + 1)
                    for i in (2 * h, 2 * h + 1):
                        last = a_.activation(prob[:, b % 2, i, :], sm[:, b % 2, i, :], ACT.Exp,
                                             bias=nmax[:, b % 2, i:i + 1], accum_out=psums[:, b % 2, i:i + 1])
                    last.then_inc(prob_ok, 1)

            exps(0)
            for b in range(B):
                act.wait_ge(gT_t, b + 1)
                a_.activation(gT[:, :, :], gT_ps, ACT.Copy).then_inc(gT_ok, 1)
                act.wait_ge(pT_t, b + 1)
                a_.activation(pTa[:, :, :], pTa_ps, ACT.Copy).then_inc(pTa_ok, 1)
                if b + 1 < B:
                    exps(b + 1)

            def turn_block(j, s):
                act.wait_ge(xgT_t, j + 1)
                a_.activation(xgT[:, s, :], xgT_ps[:, s, :], ACT.Identity,
                              bias=cols[:, BE:BE + 1], scale=cols[:, GA:GA + 1]).then_inc(xgT_ok, 1)

            def relu_half(j, s):
                act.wait_ge(h_t0, j + 1)
                for c in range(FC // 2):
                    last = a_.activation(hT[:, s, c, :], h_ps[s][0][:, c, :], ACT.Relu, bias=w1c[:, s, F + c:F + c + 1])
                last.then_inc(h_act_ok, 1)

            turn_block(0, 0)
            turn_block(1, 1)
            relu_half(0, 0)

            def expert_step(j, s, ahead2, ahead1):
                if ahead2:
                    turn_block(j + 2, (s + 2) % U)
                if ahead1:
                    relu_half(j + 1, (s + 1) % U)

            with act.Fori(0, IT - 1) as it:
                for s in range(U):
                    expert_step(U * it + s, s, True, True)
            for s in range(U):
                expert_step(U * (IT - 1) + s, s, s + 2 < U, s + 1 < U)

            for s in range(U):
                act.wait_ge(y_out[s], 16 * IT)
            for b in range(1, B, 2):
                act.dma_start(yk[:, 0, TB * b:TB * b + TB, :], yt[:, 0, TB * b:TB * b + TB, :]).then_inc(yk_in[b], 16)
                act.dma_start(yk[:, 1, TB * b:TB * b + TB, :], yt[:, 1, TB * b:TB * b + TB, :]).then_inc(yk_in[b], 16)

        @block.tensor
        def _(pe):
            t_ = nc.tensor

            def turn(b):
                pe.wait_ge(z_ok, b + 1)
                if b >= 1:
                    pe.wait_ge(xnT_ok, b)
                for i in range(TB):
                    t_.transpose(zT_ps[:, i, :], zrow[:, TB * b + i, 0, 0:H], ident[:, :])
                for i in range(TB):
                    last = t_.transpose(xT_ps[:, i, :], xn[:, TB * b + i, :], ident[:, :])
                last.then_inc(xz_t, 1)

            pe.wait_ge(ident_ok, 1)
            pe.wait_ge(rows_in, 16 * 8)
            t_.transpose(cols_ps, rows[:, :], ident[0:NROWS, 0:NROWS]).then_inc(cols_t, 1)
            turn(0)
            pe.wait_ge(wr_in, 32)
            pe.wait_ge(wa_in, 64)
            pe.wait_ge(wv_in, 16)
            pe.wait_ge(free_zero, 1)
            pe.wait_ge(consts, 1)
            for b in range(B):
                pe.wait_ge(xn2T_ok, b + 1)
                if b >= 1:
                    pe.wait_ge(slot_ok, b)
                for i in range(TB):
                    last = t_.matmul(logit_ps[:, TB * b + i, :], xn2T[:, b % 2, i * P:(i + 1) * P], wr_sb[:, :],
                                     start=True, stop=True)
                last.then_inc(logit_t, 1)
                pe.wait_ge(xnT_ok, b + 1)
                if b >= 1:
                    pe.wait_ge(k_ok, b)
                t_.matmul(bank[2][:, :], w1_sb[:, :], xnT[:, b % 2, :], start=True, stop=True).then_inc(h1_t, 1)
                if b + 1 < B:
                    turn(b + 1)
                if b >= 1:
                    pe.wait_ge(q_ok, b)
                pe.wait_ge(h1_ok, b + 1)
                t_.matmul(bank[3][:, :], w2_sb[:, :], h1T[:, :], start=True, stop=True).then_inc(m_t, 1)
                pe.wait_ge(mask_ok, b + 1)
                r = rank_ps[:, TB * b:TB * b + TB, :]
                t_.matmul(r, upper[:, :], mask[:, TB * b:TB * b + TB, :], start=True, stop=False, skip_group_check=True)
                for i in range(TB - 1):
                    t_.matmul(rank_ps[:, TB * b + i + 1:TB * b + TB, :], ones[:, :],
                              mask[:, TB * b + i:TB * b + i + 1, :].to_broadcast([P, TB - 1 - i, E]),
                              start=False, stop=False, skip_group_check=True)
                if b >= 1:
                    pe.wait_ge(before_ok, b)
                t_.matmul(r, ones[:, :], before[:, b:b + 1, :].to_broadcast([P, TB, E]),
                          start=False, stop=True, skip_group_check=True).then_inc(rank_t, 1)
                pe.wait_ge(m_ok, b + 1)
                t_.matmul(bank[2][:, :], wk_sb[:, :], mT[:, b % 2, HALF:HALF + S], start=True, stop=True).then_inc(k_t, 1)
                t_.matmul(bank[3][:, :], wq_sb[:, :], mT[:, b % 2, HALF:HALF + S], start=True, stop=True).then_inc(q_t, 1)
                if b >= 1:
                    pe.wait_ge(v_ok, b)
                for i in range(TB + 1):
                    last = t_.matmul(pv_ps[:, i, :] if i < TB else gd_ps[:, 0, :], mT[:, b % 2, i * P:(i + 1) * P],
                                     wv_sb[:, :], start=True, stop=True)
                last.then_inc(v_t, 1)

            pe.wait_ge(before_ok, B)
            pe.wait_ge(slot_ok, B)
            t_.matmul(total_ps, ones[:, :], before[:, B, :], start=True, stop=True).then_inc(total_t, 1)

            def scores(b):
                pe.wait_ge(q_ok, b + 1)
                for h in range(2):
                    if b >= 1:
                        pe.wait_ge(sm_ok, 2 * b - 1 + h)
                    for i in (2 * h, 2 * h + 1):
                        last = t_.matmul(s_ps[h][:, i % 2, 0:WIN], qT[:, b, i * P:(i + 1) * P],
                                         kT[:, b, i * P:i * P + WIN], start=True, stop=True)
                    last.then_inc(s_t, 1)

            scores(0)
            pe.wait_ge(cols_ok, 2)
            pe.wait_ge(W2_in, 16)
            for e in range(E):
                for c in range(FC):
                    last = t_.matmul(c_ps[:, e:e + 1], W2s[:, e, c, :], rb1[:, e * FC + c:e * FC + c + 1],
                                     start=(c == 0), stop=(c == FC - 1))
            last.then_inc(c_t, 1)
            pe.wait_ge(v_ok, B)
            for b in range(B):
                if b + 1 < B:
                    scores(b + 1)
                if b == 0:
                    pe.wait_ge(d_ready, 1)
                    t_.transpose(d_ps, dT[:, :], ident[:, :]).then_inc(dT_t, 1)
                    pe.wait_ge(table, 1)
                pe.wait_ge(gfull_ok, b + 1)
                if b >= 1:
                    pe.wait_ge(gT_ok, b)
                for i in range(TB):
                    last = t_.transpose(gT_ps[:, i, :], gfull[:, TB * b + i, :], ident[:, :])
                last.then_inc(gT_t, 1)
                pe.wait_ge(prob_ok, 2 * b + 2)
                if b >= 1:
                    pe.wait_ge(pTa_ok, b)
                    pe.wait_ge(pTb_ok, b)
                for i in range(TB):
                    t_.transpose(pTa_ps[:, i, :], prob[:, b % 2, i, 0:P], ident[:, :])
                    last = t_.transpose(pTb_ps[0:CH, i, :], prob[:, b % 2, i, P:WIN], ident[:, :])
                last.then_inc(pT_t, 1)
                if b == 0:
                    pe.wait_ge(d_ok, 1)
                pe.wait_ge(gT_ok, b + 1)
                if b >= 1:
                    pe.wait_ge(acc_ok, b)
                for i in range(TB):
                    last = t_.matmul(gd_ps[:, i, :], gT[:, i, :], d_rows[:, :], start=True, stop=True)
                last.then_inc(gd_t, 1)
                pe.wait_ge(pTa_ok, b + 1)
                pe.wait_ge(pTb_ok, b + 1)
                for i in range(TB):
                    t_.matmul(pv_ps[:, i, :], pTa[:, i, :], v[:, b, i, :], start=True, stop=False)
                    last = t_.matmul(pv_ps[:, i, :], pTb[:, i, :], v[0:CH, b, i + 1, :], start=False, stop=True)
                last.then_inc(pv_t, 1)

            def turn_block(j, s, value):
                pe.wait_ge(xg_in[s], value)
                if not isinstance(j, int) or j >= 1:
                    pe.wait_ge(xgT_ok, j)
                t_.transpose(xgT_ps[:, s, :], xg[:, s, 0:H], ident[:, :]).then_inc(xgT_t, 1)

            def first(j, s):
                pe.wait_ge(xgT_ok, j + 1)
                pe.wait_ge(w1c_ok, j + 1)
                for half, done in enumerate((h_t0, h_t1)):
                    for c in range(FC // 2):
                        f = half * FC // 2 + c
                        last = t_.matmul(h_ps[s][half][:, c, :], w1c[:, s, f * P:(f + 1) * P], xgT[:, s, :],
                                         start=True, stop=True)
                    last.then_inc(done, 1)

            def second(j, s):
                e = pe.value_load(expert_i[0:1, bass.ds(j, 1)], min_val=0, max_val=E - 1)
                pe.wait_ge(h_act_ok, j + 1)
                pe.wait_ge(h_dve_ok, j + 1)
                if not isinstance(j, int) or j >= 1:
                    pe.wait_ge(y_ok, j)
                for c in range(FC):
                    last = t_.matmul(y_ps[:, s, :], hT[:, s, c, :],
                                     W2s[:, bass.ds(e, 1), c, :].rearrange("p o h -> p (o h)"),
                                     start=(c == 0), stop=(c == FC - 1))
                last.then_inc(y_t, 1)

            pe.wait_ge(table_ok, 1)
            turn_block(0, 0, 16)
            turn_block(1, 1, 16)
            first(0, 0)
            pe.wait_ge(acc_ok, B)

            def expert_step(it, s, ahead2, ahead1):
                j = U * it + s
                if ahead2:
                    turn_block(j + 2, (s + 2) % U, 16 * it + 16 * ((s + 2) // U) + 16)
                if ahead1:
                    first(j + 1, (s + 1) % U)
                second(j, s)

            with pe.Fori(0, IT - 1) as it:
                for s in range(U):
                    expert_step(it, s, True, True)
            for s in range(U):
                expert_step(IT - 1, s, s + 2 < U, s + 1 < U)


_INS = ['L0_attn_x', 'L0_attn_nm_w1', 'L0_attn_nm_b1', 'L0_attn_nm_w2', 'L0_attn_nm_b2', 'L0_attn_q_w',
        'L0_attn_q_b', 'L0_attn_k_w', 'L0_attn_k_b', 'L0_attn_v_w', 'L0_attn_v_b', 'L0_ffn_gamma', 'L0_ffn_beta',
        'L0_ffn_Wr', 'L0_ffn_br', 'L0_ffn_W1', 'L0_ffn_b1', 'L0_ffn_W2', 'L0_ffn_b2']
_OUTS = [((4, 512, 128), 'float32')]


def kernel(**inputs):
    import numpy as _np
    import concourse.bacc as _bacc
    from concourse import mybir as _mybir
    from concourse.bass_utils import run_bass_kernel_spmd as _run

    nc = _bacc.Bacc("TRN2", target_bir_lowering=False, num_devices=1)
    arrays, args = {}, []
    for name in _INS:
        a = _np.ascontiguousarray(inputs[name])
        arrays[f"in_{name}_dram"] = a
        args.append(nc.dram_tensor(f"in_{name}_dram", a.shape, _mybir.dt.from_np(a.dtype), kind="ExternalInput").ap())
    for i, (shape, dtype) in enumerate(_OUTS):
        dt = _mybir.dt.from_np(_np.dtype(dtype))
        args.append(nc.dram_tensor(f"out_{i}_dram", shape, dt, kind="ExternalOutput").ap())
    build(nc, *args)
    r = _run(nc, [arrays], core_ids=[0])
    return r.results[0]["out_0_dram"]
```

```python
import concourse.bass as bass
from concourse import mybir
from contextlib import ExitStack


def build(nc, x, nm_w1, nm_b1, nm_w2, nm_b2, q_w, q_b, k_w, k_b, v_w, v_b,
          gamma, beta, Wr, br, W1, b1, W2, b2, out):
    f32 = mybir.dt.float32
    i32 = mybir.dt.int32
    u32 = mybir.dt.uint32
    bf16 = mybir.dt.bfloat16
    ALU = mybir.AluOpType
    ACT = mybir.ActivationFunctionType
    AX = mybir.AxisListType.X

    P = 128
    B, S, H = x.shape
    E, _, F = W1.shape
    K = 2
    N = B * S
    TB = S // P
    NT = N // P
    FC = F // P
    HALF = 32
    WIN = P + 2 * HALF
    CH = WIN - P
    PADK = (TB + 1) * P
    EPS = 1e-5
    SCALE = float(H) ** -0.5
    NEG = -1e30
    ROW = H + 2
    GATE, DEST = H, H + 1
    REG = N + P
    MAXBLK = (N * K - E) // P + E
    POOL_SUMS = (2, 3)
    NOWHERE = 1 << 20
    U = 3
    IT = MAXBLK // U
    WX = F + FC + H
    FA = 3
    assert H == P and TB == 4 and E % TB == 0 and MAXBLK == U * IT and N * K // P >= E

    xt = x.rearrange("b (t p) h -> p (b t) h", p=P)
    ot = out.rearrange("b (t p) h -> p (b t) h", p=P)
    disp = nc.dram_tensor("disp", [E * REG + P, ROW], f32, kind="Internal").ap()
    ysel = nc.dram_tensor("ysel", [K * N, H], f32, kind="Internal").ap()
    yt = ysel.rearrange("(k t p) h -> p k t h", k=K, p=P)

    ctx = ExitStack()
    with ctx:
        def sb(name, shape, dt=f32):
            return ctx.enter_context(nc.sbuf_tensor(name, shape, dt))

        def sem(name):
            return ctx.enter_context(nc.semaphore(name))

        ident = sb("ident", [P, P])
        upper = sb("upper", [P, P], bf16)
        ones = sb("ones", [P, P], bf16)
        ones_e = sb("ones_e", [P, P])
        minus_half = sb("minus_half", [P, TB])
        identb = sb("identb", [P, P], bf16)
        band = sb("band", [P, TB, WIN], bf16)
        iota_e = sb("iota_e", [P, E])
        region = sb("region", [P, E])
        iota_j = sb("iota_j", [1, MAXBLK])
        iota_128 = sb("iota_128", [1, NT])
        one_row = sb("one_row", [1, E])
        warm = sb("warm", [1, 1])
        padrow = sb("padrow", [P, ROW])
        w1_sb = sb("w1_sb", [H, H])
        w2_sb = sb("w2_sb", [H, H])
        wkqv = sb("wkqv", [H, 3, H])
        w2T = sb("w2T", [H, H])
        fold = sb("fold", [H, 3, H])
        wr_sb = sb("wr_sb", [H, E])
        br_bc = sb("br_bc", [P, E])
        vb_bc = sb("vb_bc", [P, H])
        NROWS = E * FC + E + 6
        B2, NB1, NB2, QB, KB, GA, BE = E * FC, E * FC + E, NROWS - 5, NROWS - 4, NROWS - 3, NROWS - 2, NROWS - 1
        rows = sb("rows", [NROWS, H])
        cols = sb("cols", [P, NROWS])
        kqb = sb("kqb", [P, 2])
        qbs = sb("qbs", [P, 1])
        W1x = sb("W1x", [H, E, WX])
        W2s = sb("W2s", [P, E, FC, H])
        x_sb = sb("x_sb", [P, NT, H])
        xn = sb("xn", [P, NT, H])
        stats = sb("stats", [P, 2, NT, 6])
        mv = sb("mv", [P, 2, NT, 2])
        veps = sb("veps", [P, 2, NT])
        rstd = sb("rstd", [P, 2, NT])
        negmean = sb("negmean", [P, NT])
        nmr = sb("nmr", [P, NT])
        zrow = sb("zrow", [P, NT, K, ROW])
        lg = sb("lg", [P, NT, E])
        best = sb("best", [P, NT, 8])
        bidx = sb("bidx", [P, NT, 8], u32)
        bidxf = sb("bidxf", [P, NT, K])
        rel = sb("rel", [P, NT, E])
        erel = sb("erel", [P, NT, E])
        esum = sb("esum", [P, NT])
        einv = sb("einv", [P, NT])
        gates = sb("gates", [P, NT, K])
        oh = sb("oh", [P, NT, K, E])
        mask = sb("mask", [P, NT, E], bf16)
        msum = sb("msum", [P, B, E], bf16)
        before = sb("before", [P, B + 1, E], bf16)
        slot = sb("slot", [P, NT, E])
        ohslot = sb("ohslot", [P, NT, K, E])
        pos = sb("pos", [P, NT, K], i32)
        over = sb("over", [1, E, NT])
        nblk = sb("nblk", [1, E])
        count_i = sb("count_i", [1, E], i32)
        incl = sb("incl", [1, E])
        past = sb("past", [1, MAXBLK, E])
        pastn = sb("pastn", [1, MAXBLK, E])
        eb = sb("eb", [1, MAXBLK])
        excl = sb("excl", [1, MAXBLK])
        jrel = sb("jrel", [1, MAXBLK])
        startf = sb("startf", [1, MAXBLK])
        start_i = sb("start_i", [1, MAXBLK], i32)
        expert_i = sb("expert_i", [1, MAXBLK], i32)
        xnT = sb("xnT", [H, 2, S])
        xn2T = sb("xn2T", [H, 2, S])
        h1T = sb("h1T", [H, 2, PADK])
        qT = sb("qT", [H, B, S])
        kT = sb("kT", [H, B, PADK])
        v = sb("v", [P, B, TB + 1, H])
        nmax = sb("nmax", [P, 2, TB])
        prob = sb("prob", [P, 2, TB, WIN])
        psums = sb("psums", [P, 2, TB])
        pinv = sb("pinv", [P, 2, TB])
        pTa = sb("pTa", [P, TB, P])
        pTb = sb("pTb", [CH, TB, P])
        acc = sb("acc", [P, NT, H])
        rb1 = sb("rb1", [P, E * FC])
        cw = sb("cw", [P, E, H])
        b2_sum = sb("b2_sum", [P, H])
        c_tot = sb("c_tot", [P, H])
        xg = sb("xg", [P, U, ROW])
        meta_g = sb("meta_g", [P, MAXBLK])
        meta_d = sb("meta_d", [P, MAXBLK], i32)
        yd = sb("yd", [P, U, H])
        xgT = sb("xgT", [H, U, P])
        w1c = sb("w1c", [H, U, WX])
        hT = sb("hT", [P, U, FC, P])
        ys = sb("ys", [P, MAXBLK, H])
        yk = sb("yk", [P, K, NT, H])

        bank = [ctx.enter_context(nc.psum_tensor(f"bank{i}", [P, 512], f32)) for i in range(8)]

        def tiles(i):
            return bank[i][:, :].rearrange("p (t c) -> p t c", t=TB)

        s_ps = [bank[i][:, :].rearrange("p (t c) -> p t c", t=2) for i in (0, 1)]
        h1_ps, k_ps = bank[2], bank[2]
        xT_ps, zT_ps, q_ps = tiles(3), tiles(3), bank[3]
        logit_ps = bank[4][:, 0:NT * E].rearrange("p (t e) -> p t e", e=E)
        rank_ps = bank[4][:, NT * E:2 * NT * E].rearrange("p (t e) -> p t e", e=E)
        total_ps = bank[4][:, 2 * NT * E:2 * NT * E + E]
        pv_ps, v4_ps = tiles(5), bank[6][:, 0:H]
        pTa_ps, pTb_ps = tiles(7), tiles(6)
        cw_ps = tiles(7)
        fold_ps = bank[0][:, 0:3 * H].rearrange("p (a c) -> p a c", a=3)
        kqb_ps = bank[1][:, 0:2]
        w2T_ps = bank[5][:, 0:H]
        vb_ps, b2_ps = bank[6][:, 0:H], bank[6][:, H:2 * H]
        cols_ps = bank[7][:, 0:NROWS]
        h_ps = [[tiles(i) for i in pair] for pair in ((0, 1), (2, 4), (5, 6))]
        xgT_ps = tiles(3)
        y_ps = tiles(7)

        x_in = [sem(f"x_in{b}") for b in range(B)]
        rows_in = sem("rows_in")
        b_in = sem("b_in")
        w1_in = sem("w1_in")
        w2_in = sem("w2_in")
        wr_in = sem("wr_in")
        br_in = sem("br_in")
        wa_in = sem("wa_in")
        vb_in = sem("vb_in")
        W1_in = sem("W1_in")
        W2_in = sem("W2_in")
        pads_out = sem("pads_out")
        sent = sem("sent")
        xg_in = [sem(f"xg_in{s}") for s in range(U)]
        y_out = sem("y_out")
        yk_in = [sem(f"yk_in{b}") for b in range(B)]
        stored = sem("stored")
        (consts, routing_consts, ident_ok, cols_t, cols_ok, stat1, var1, rstd1, xn_ok, stat2, var2, rstd2, nmr_ok, z_ok,
         xT_t, zT_t, xnT_ok, xn2T_ok, logit_t, lg_ok, best_ok, rel_ok, erel_ok, esum_ok, einv_ok, gate_ok,
         idx_ok, idxf_ok, oh_ok, mask_ok, msum_ok, before_ok, rank_t, slot_ok, ohslot_ok, pos_ok,
         w2T_t, w2T_ok, fold_t, fold_ok, kqb_t, kqb_ok, vb_ok, h1_t, h1_ok, k_t, k_ok, q_t, q_ok, v_t, v_ok,
         total_t, table, counts_ok, table_ok, s_t, nmax_ok, prob_ok, pT_t, pTa_ok, pTb_ok, pinv_ok,
         pv_t, acc_ok, res_ok, c_t, c_ok, cstep, d_ok,
         xgT_t, xgT_ok, meta_ok, w1b_ok, w1c_ok, h_t0, h_t1, h_act_ok, h_dve_ok, y_t, yd_ok, y_ok, sum_ok, out_ok,
         const_step, free_zero, one_ok, psum_ok) = [sem(n) for n in (
             "consts routing_consts ident_ok cols_t cols_ok stat1 var1 rstd1 xn_ok stat2 var2 rstd2 nmr_ok z_ok "
             "xT_t zT_t xnT_ok xn2T_ok logit_t lg_ok best_ok rel_ok erel_ok esum_ok einv_ok gate_ok "
             "idx_ok idxf_ok oh_ok mask_ok msum_ok before_ok rank_t slot_ok ohslot_ok pos_ok "
             "w2T_t w2T_ok fold_t fold_ok kqb_t kqb_ok vb_ok h1_t h1_ok k_t k_ok q_t q_ok v_t v_ok "
             "total_t table counts_ok table_ok s_t nmax_ok prob_ok pT_t pTa_ok pTb_ok pinv_ok "
             "pv_t acc_ok res_ok c_t c_ok cstep d_ok "
             "xgT_t xgT_ok meta_ok w1b_ok w1c_ok h_t0 h_t1 h_act_ok h_dve_ok y_t yd_ok y_ok sum_ok out_ok "
             "const_step free_zero one_ok psum_ok").split()]

        block = ctx.enter_context(nc.Block())

        def table_values(table_row, j, engine, top):
            return nc.values_load_multi_w_load_instructions(
                table_row[0:1, bass.ds(j, U)], engines=[engine], min_val=0, max_val=top,
                skip_runtime_bounds_check_because="the table's entries are whole numbers from 0 to top, by a min")[1]

        @block.sync
        def _(sp):
            def load_x(b):
                sp.dma_start(x_sb[:, TB * b:TB * b + TB, :], xt[:, TB * b:TB * b + TB, :]).then_inc(x_in[b], 16)

            load_x(0)
            sp.dma_start(w1_sb[:, :], nm_w1).then_inc(w1_in, 16)
            load_x(1)
            sp.dma_start(w2_sb[:, :], nm_w2).then_inc(w2_in, 16)
            for i, w in enumerate((k_w, q_w, v_w)):
                sp.dma_start(wkqv[:, i, :], w).then_inc(wa_in, 16)
            sp.dma_start(wr_sb[:, :], Wr).then_inc(wr_in, 16)
            sp.dma_start(vb_bc[:, :], v_b.partition_broadcast(P)).then_inc(vb_in, 16)
            sp.dma_start(br_bc[:, :], br.partition_broadcast(P)).then_inc(br_in, 16)
            load_x(2)
            sp.dma_start(W2s[:, :, :, :], W2.rearrange("e (c p) h -> p e c h", p=P)).then_inc(W2_in, 16)
            load_x(3)
            sp.dma_start(W1x[:, :, 0:F], W1.rearrange("e h f -> h e f")).then_inc(W1_in, 16)
            sp.wait_ge(routing_consts, 1)
            sp.dma_start(disp[E * REG:E * REG + P, :], padrow[:, :]).then_inc(pads_out, 16)
            sp.wait_ge(counts_ok, 1)
            for e in range(E):
                n = sp.value_load(count_i[0:1, e:e + 1], min_val=0, max_val=N)
                sp.dma_start(disp[bass.ds(n + e * REG, P), :], padrow[:, :]).then_inc(pads_out, 16)
            sp.wait_ge(pads_out, 16 * (E + 1))
            sp.wait_ge(sent, 16 * NT * K)

            def load_block(r, s):
                sp.dma_start(xg[:, s, :], disp[bass.ds(r, P), :]).then_inc(xg_in[s], 16)

            sp.wait_ge(table_ok, 1)
            starts = table_values(start_i, 0, mybir.EngineType.SP, E * REG)
            for s in range(U):
                load_block(starts[s], s)
            with sp.Fori(1, IT) as it:
                starts = table_values(start_i, U * it, mybir.EngineType.SP, E * REG)
                for s in range(U):
                    sp.wait_ge(xgT_t, U * it - U + s + 1)
                    sp.wait_ge(meta_ok, U * it - U + s + 1)
                    load_block(starts[s], s)

            sp.wait_ge(y_out, 16 * MAXBLK)
            for b in range(0, B, 2):
                sp.dma_start(yk[:, 0, TB * b:TB * b + TB, :], yt[:, 0, TB * b:TB * b + TB, :]).then_inc(yk_in[b], 16)
                sp.dma_start(yk[:, 1, TB * b:TB * b + TB, :], yt[:, 1, TB * b:TB * b + TB, :]).then_inc(yk_in[b], 16)
            for b in range(B):
                sp.wait_ge(out_ok, b + 1)
                sp.dma_start(ot[:, TB * b:TB * b + TB, :], acc[:, TB * b:TB * b + TB, :]).then_inc(stored, 16)
            sp.wait_ge(stored, 16 * B)

        @block.gpsimd
        def _(pool):
            g = nc.gpsimd
            g.memset(ident[:, :], 0.0)
            g.memset(minus_half[:, :], -0.5).then_inc(const_step, 1)
            pool.wait_ge(const_step, 1)
            g.affine_select(out=ident[:, :], in_=ident[:, :], compare_op=ALU.not_equal, fill=1.0,
                            base=0, pattern=[[-1, P]], channel_multiplier=1).then_inc(ident_ok, 1)

            g.dma_start(rows[0:B2, :], b1.rearrange("e (c p) -> (e c) p", p=P)).then_inc(b_in, 16)
            g.dma_start(rows[B2:B2 + E, :], b2).then_inc(b_in, 16)

            g.memset(identb[:, :], 0.0)
            g.memset(upper[:, :], 0.0)
            g.memset(band[:, :, :], 0.0)
            g.memset(padrow[:, :], 0.0).then_inc(const_step, 1)

            def small_constants():
                g.iota(iota_e[:, :], pattern=[[1, E]], base=0, channel_multiplier=0,
                       allow_small_or_imprecise_dtypes=True)
                g.iota(region[:, :], pattern=[[REG, E]], base=0, channel_multiplier=0,
                       allow_small_or_imprecise_dtypes=True)
                g.iota(iota_j[:, :], pattern=[[1, MAXBLK]], base=0, channel_multiplier=0,
                       allow_small_or_imprecise_dtypes=True)
                g.iota(iota_128[:, :], pattern=[[P, NT]], base=0, channel_multiplier=0,
                       allow_small_or_imprecise_dtypes=True)
                g.iota(zrow[:, :, :, DEST:DEST + 1].rearrange("p t k o -> p t (k o)"),
                       pattern=[[P, NT], [N, K]], base=0, channel_multiplier=1,
                       allow_small_or_imprecise_dtypes=True)
                pool.wait_ge(const_step, 2)
                g.memset(padrow[:, DEST:DEST + 1], float(NOWHERE))
                g.affine_select(out=upper[:, :], in_=upper[:, :], compare_op=ALU.is_ge, fill=1.0,
                                base=0, pattern=[[-1, P]], channel_multiplier=1).then_inc(routing_consts, 1)

            def band_constants():
                g.affine_select(out=identb[:, :], in_=identb[:, :], compare_op=ALU.not_equal, fill=1.0,
                                base=0, pattern=[[-1, P]], channel_multiplier=1)
                g.affine_select(out=band[:, :, :], in_=band[:, :, :], compare_op=ALU.is_ge, fill=NEG,
                                base=0, pattern=[[0, TB], [1, WIN]], channel_multiplier=-1).then_inc(const_step, 1)
                pool.wait_ge(const_step, 3)
                g.affine_select(out=band[:, :, :], in_=band[:, :, :], compare_op=ALU.is_ge, fill=NEG,
                                base=2 * HALF, pattern=[[0, TB], [-1, WIN]], channel_multiplier=1).then_inc(const_step, 1)
                pool.wait_ge(const_step, 4)
                g.memset(band[:, 0, 0:HALF], NEG)
                g.memset(band[:, TB - 1, HALF + P:WIN], NEG).then_inc(consts, 1)

            def inverse_root(l, b, var, done):
                pool.wait_ge(var, b + 1)
                g.tensor_tensor(rstd[:, l, TB * b:TB * b + TB], veps[:, l, TB * b:TB * b + TB],
                                minus_half[:, :], ALU.pow).then_inc(done, 1)
                if l == 1:
                    pool.wait_ge(done, b + 1)
                    g.tensor_tensor(nmr[:, TB * b:TB * b + TB], negmean[:, TB * b:TB * b + TB],
                                    rstd[:, 1, TB * b:TB * b + TB], ALU.mult).then_inc(nmr_ok, 1)

            def send(b, k):
                for t in range(TB * b, TB * b + TB):
                    g.indirect_dma_start(disp[:, :], bass.IndirectOffsetOnAxis(ap=pos[:, t, k:k + 1], axis=0),
                                         zrow[:, t, k, :], None).then_inc(sent, 16)

            inverse_root(0, 0, var1, rstd1)
            small_constants()
            inverse_root(1, 0, var2, rstd2)
            inverse_root(0, 1, var1, rstd1)
            band_constants()
            inverse_root(0, 2, var1, rstd1)
            inverse_root(1, 1, var2, rstd2)
            inverse_root(1, 2, var2, rstd2)
            for b in range(B):
                if b == 1:
                    inverse_root(0, B - 1, var1, rstd1)
                pool.wait_ge(pos_ok, b + 1)
                pool.wait_ge(gate_ok, b + 1)
                send(b, 0)
                if b == 1:
                    inverse_root(1, B - 1, var2, rstd2)
                send(b, 1)

            def send_back(j):
                pool.wait_ge(y_ok, j + 1)
                pool.wait_ge(meta_ok, j + 1)
                g.indirect_dma_start(ysel[:, :], bass.IndirectOffsetOnAxis(ap=meta_d[:, j:j + 1], axis=0),
                                     ys[:, j, :], None, bounds_check=K * N - 1, oob_is_err=False).then_inc(y_out, 16)

            def residual(n):
                b, what, half = n // 6, n % 6 // 2, n % 2
                ts = slice(TB * b + TB // 2 * half, TB * b + TB // 2 * half + TB // 2)
                part = (x_sb[:, ts, :], xn[:, ts, :], vb_bc[:, :].unsqueeze(1).to_broadcast([P, TB // 2, H]))[what]
                if n == 0:
                    pool.wait_ge(acc_ok, B)
                elif n >= 2:
                    pool.wait_ge(res_ok, n - 1)
                g.tensor_tensor(acc[:, ts, :], acc[:, ts, :], part, ALU.add).then_inc(res_ok, 1)

            for j in range(MAXBLK):
                send_back(j)
                if j < 6 * B:
                    residual(j)

            for b in POOL_SUMS:
                ts = slice(TB * b, TB * b + TB)
                pool.wait_ge(yk_in[b], 32)
                pool.wait_ge(res_ok, 6 * B)
                g.tensor_tensor(acc[:, ts, :], acc[:, ts, :], yk[:, 0, ts, :], ALU.add).then_inc(psum_ok, 1)

        @block.vector
        def _(dve):
            v_ = nc.vector

            def norm1_stats(b):
                dve.wait_ge(x_in[b], 16)
                for t in range(TB * b, TB * b + TB):
                    last = v_.bn_stats(stats[:, 0, t, :], x_sb[:, t, :])
                last.then_inc(stat1, 1)
                dve.wait_ge(stat1, 2 * b + 1)
                for t in range(TB * b, TB * b + TB):
                    last = v_.bn_aggr(mv[:, 0, t, :], stats[:, 0, t, :])
                last.then_inc(stat1, 1)
                dve.wait_ge(stat1, 2 * b + 2)
                v_.tensor_scalar(veps[:, 0, TB * b:TB * b + TB], mv[:, 0, TB * b:TB * b + TB, 1], EPS, None,
                                 ALU.add).then_inc(var1, 1)

            def norm1_apply(b):
                dve.wait_ge(rstd1, b + 1)
                for t in range(TB * b, TB * b + TB):
                    last = v_.tensor_scalar(xn[:, t, :], x_sb[:, t, :], mv[:, 0, t, 0:1], rstd[:, 0, t:t + 1],
                                            ALU.subtract, ALU.mult)
                last.then_inc(xn_ok, 1)
                dve.wait_ge(xn_ok, b + 1)
                for t in range(TB * b, TB * b + TB):
                    last = v_.bn_stats(stats[:, 1, t, :], xn[:, t, :])
                last.then_inc(stat2, 1)
                dve.wait_ge(stat2, 2 * b + 1)
                for t in range(TB * b, TB * b + TB):
                    last = v_.bn_aggr(mv[:, 1, t, :], stats[:, 1, t, :])
                last.then_inc(stat2, 1)
                dve.wait_ge(stat2, 2 * b + 2)
                v_.tensor_scalar(negmean[:, TB * b:TB * b + TB], mv[:, 1, TB * b:TB * b + TB, 0], -1.0, None, ALU.mult)
                v_.tensor_scalar(veps[:, 1, TB * b:TB * b + TB], mv[:, 1, TB * b:TB * b + TB, 1], EPS, None,
                                 ALU.add).then_inc(var2, 1)

            def choose(b):
                ts = slice(TB * b, TB * b + TB)
                dve.wait_ge(logit_t, b + 1)
                v_.tensor_tensor(lg[:, ts, :], logit_ps[:, ts, :], br_bc[:, :].unsqueeze(1).to_broadcast([P, TB, E]),
                                 ALU.add).then_inc(lg_ok, 1)
                dve.wait_ge(lg_ok, b + 1)
                for t in range(TB * b, TB * b + TB):
                    last = v_.max(best[:, t, :], lg[:, t, :])
                last.then_inc(best_ok, 1)
                dve.wait_ge(best_ok, b + 1)
                v_.tensor_tensor(rel[:, ts, :], best[:, ts, :], best[:, ts, 0:1].to_broadcast([P, TB, E]),
                                 ALU.subtract).then_inc(rel_ok, 1)
                for t in range(TB * b, TB * b + TB):
                    last = v_.max_index(bidx[:, t, :], best[:, t, :], lg[:, t, :])
                last.then_inc(idx_ok, 1)
                dve.wait_ge(idx_ok, b + 1)
                v_.tensor_copy(bidxf[:, ts, :], bidx[:, ts, 0:K]).then_inc(idxf_ok, 1)
                dve.wait_ge(idxf_ok, b + 1)
                v_.tensor_tensor(oh[:, ts, :, :].rearrange("p t k e -> p (t k) e"),
                                 iota_e[:, :].unsqueeze(1).to_broadcast([P, TB * K, E]),
                                 bidxf[:, ts, :].rearrange("p t k -> p (t k)").unsqueeze(2).to_broadcast([P, TB * K, E]),
                                 ALU.is_equal).then_inc(oh_ok, 1)
                dve.wait_ge(oh_ok, b + 1)
                v_.tensor_tensor(mask[:, ts, :], oh[:, ts, 0, :], oh[:, ts, 1, :], ALU.add).then_inc(mask_ok, 1)
                dve.wait_ge(mask_ok, b + 1)
                with nc.allow_low_precision("counts up to 16 are exact in bfloat16"):
                    v_.tensor_reduce(msum[:, b, :], mask[:, ts, :].rearrange("p t e -> p e t"), AX,
                                     ALU.add).then_inc(msum_ok, 1)
                dve.wait_ge(msum_ok, b + 1)
                v_.tensor_tensor(before[:, b + 1, :], before[:, b, :], msum[:, b, :], ALU.add).then_inc(before_ok, 1)

            def weights(b):
                ts = slice(TB * b, TB * b + TB)
                dve.wait_ge(erel_ok, b + 1)
                v_.tensor_reduce(esum[:, ts], erel[:, ts, :], AX, ALU.add).then_inc(esum_ok, 1)
                dve.wait_ge(esum_ok, b + 1)
                v_.reciprocal(einv[:, ts], esum[:, ts]).then_inc(einv_ok, 1)
                dve.wait_ge(einv_ok, b + 1)
                v_.tensor_tensor(zrow[:, ts, :, GATE], erel[:, ts, 0:K],
                                 einv[:, ts].unsqueeze(2).to_broadcast([P, TB, K]), ALU.mult).then_inc(gate_ok, 1)

            def place(b):
                ts = slice(TB * b, TB * b + TB)
                dve.wait_ge(rank_t, b + 1)
                v_.tensor_tensor(slot[:, ts, :], rank_ps[:, ts, :], region[:, :].unsqueeze(1).to_broadcast([P, TB, E]),
                                 ALU.add).then_inc(slot_ok, 1)
                dve.wait_ge(slot_ok, b + 1)
                v_.tensor_tensor(ohslot[:, ts, :, :], oh[:, ts, :, :],
                                 slot[:, ts, :].unsqueeze(2).to_broadcast([P, TB, K, E]), ALU.mult).then_inc(ohslot_ok, 1)
                dve.wait_ge(ohslot_ok, b + 1)
                with nc.allow_low_precision("whole numbers below 2 ** 24, summed in float32"):
                    v_.tensor_reduce(pos[:, ts, :].rearrange("p t k -> p (t k)"),
                                     ohslot[:, ts, :, :].rearrange("p t k e -> p (t k) e"), AX,
                                     ALU.add).then_inc(pos_ok, 1)

            def maxima(b):
                for h in range(2):
                    dve.wait_ge(s_t, 2 * b + h + 1)
                    v_.tensor_reduce(nmax[:, b % 2, 2 * h:2 * h + 2], s_ps[h][:, :, 0:WIN], AX, ALU.max,
                                     negate=True).then_inc(nmax_ok, 1)

            v_.memset(one_row[:, :], 1.0).then_inc(one_ok, 1)
            v_.memset(before[:, 0, :], 0.0)
            v_.memset(ones[:, :], 1.0)
            v_.memset(ones_e[:, :], 1.0)
            v_.memset(h1T[:, :, 0:HALF], 0.0)
            v_.memset(h1T[:, :, HALF + S:PADK], 0.0)
            v_.memset(kT[:, :, 0:HALF], 0.0)
            v_.memset(kT[:, :, HALF + S:PADK], 0.0).then_inc(free_zero, 1)
            norm1_stats(0)
            norm1_apply(0)
            norm1_stats(1)
            norm1_stats(2)
            norm1_apply(1)
            dve.wait_ge(vb_in, 16)
            dve.wait_ge(kqb_t, 1)
            v_.tensor_tensor(vb_bc[:, :], vb_bc[:, :], vb_ps, ALU.add)
            v_.tensor_copy(b2_sum[:, :], b2_ps).then_inc(vb_ok, 1)
            norm1_apply(2)
            dve.wait_ge(routing_consts, 1)
            dve.wait_ge(br_in, 16)

            def table_of_blocks():
                steps = [0]

                def after(ins):
                    steps[0] += 1
                    ins.then_inc(table, 1)
                    dve.wait_ge(table, steps[0])

                dve.wait_ge(total_t, 1)
                v_.tensor_copy(count_i[:, :], total_ps[0:1, :]).then_inc(counts_ok, 1)
                after(v_.tensor_tensor(over[:, :, :], total_ps[0:1, :].unsqueeze(2).to_broadcast([1, E, NT]),
                                       iota_128[:, :].unsqueeze(1).to_broadcast([1, E, NT]), ALU.is_gt))
                after(v_.tensor_reduce(nblk[:, :], over[:, :, :], AX, ALU.add))
                after(v_.tensor_tensor_scan(incl[:, :], one_row[:, :], nblk[:, :], 0.0, ALU.mult, ALU.add))
                after(v_.tensor_tensor(past[:, :, :], iota_j[:, :].unsqueeze(2).to_broadcast([1, MAXBLK, E]),
                                       incl[:, :].unsqueeze(1).to_broadcast([1, MAXBLK, E]), ALU.is_ge))
                after(v_.tensor_tensor(pastn[:, :, :], past[:, :, :],
                                       nblk[:, :].unsqueeze(1).to_broadcast([1, MAXBLK, E]), ALU.mult))
                v_.tensor_reduce(eb[:, :], past[:, :, :], AX, ALU.add)
                after(v_.tensor_reduce(excl[:, :], pastn[:, :, :], AX, ALU.add))
                v_.tensor_scalar(expert_i[:, :], eb[:, :], float(E - 1), None, ALU.min)
                after(v_.tensor_tensor(jrel[:, :], iota_j[:, :], excl[:, :], ALU.subtract))
                after(v_.tensor_scalar(startf[:, :], eb[:, :], float(REG), None, ALU.mult))
                after(v_.scalar_tensor_tensor(startf[:, :], jrel[:, :], float(P), startf[:, :], ALU.mult, ALU.add))
                v_.tensor_scalar(start_i[:, :], startf[:, :], float(E * REG), None, ALU.min).then_inc(table_ok, 1)

            def constant_rows():
                dve.wait_ge(c_ok, E // TB)
                v_.tensor_reduce(c_tot[:, :], cw[:, :, :].rearrange("p e h -> p h e"), AX, ALU.add).then_inc(cstep, 1)
                dve.wait_ge(cstep, 1)
                v_.tensor_tensor(c_tot[:, :], c_tot[:, :], b2_sum[:, :], ALU.add).then_inc(cstep, 1)
                dve.wait_ge(cstep, 2)
                v_.tensor_tensor(W1x[:, :, F + FC:WX], c_tot[:, :].unsqueeze(1).to_broadcast([P, E, H]), cw[:, :, :],
                                 ALU.subtract).then_inc(d_ok, 1)

            def probs_turned(b):
                dve.wait_ge(pT_t, b + 1)
                v_.tensor_copy(pTb[:, :, :], pTb_ps[0:CH, :, :]).then_inc(pTb_ok, 1)
                v_.reciprocal(pinv[:, b % 2, :], psums[:, b % 2, :]).then_inc(pinv_ok, 1)

            def attended(b):
                dve.wait_ge(pinv_ok, b + 1)
                dve.wait_ge(pv_t, b + 1)
                v_.tensor_tensor(acc[:, TB * b:TB * b + TB, :], pv_ps,
                                 pinv[:, b % 2, :].unsqueeze(2).to_broadcast([P, TB, H]), ALU.mult).then_inc(acc_ok, 1)

            choose(0)
            norm1_stats(3)
            weights(0)
            place(0)
            for b in range(B):
                if b + 1 < B:
                    choose(b + 1)
                if b >= 1:
                    probs_turned(b - 1)
                if b + 1 < B:
                    weights(b + 1)
                    place(b + 1)
                if b == 0:
                    norm1_apply(3)
                if b >= 1:
                    attended(b - 1)
                if b == 1:
                    constant_rows()
                maxima(b)
                if b == B - 2:
                    table_of_blocks()
            probs_turned(B - 1)
            attended(B - 1)

            def take_w1(j, s, e):
                if not isinstance(j, int) or j >= U:
                    dve.wait_ge(yd_ok, j - U + 1)
                v_.tensor_copy(w1c[:, s, :], W1x[:, bass.ds(e, 1), :].rearrange("p o f -> p (o f)")).then_inc(w1c_ok, 1)

            def relu_part(j, s):
                dve.wait_ge(h_t1, j + 1)
                dve.wait_ge(w1c_ok, j + 1)
                for c in range(FA, FC):
                    last = v_.tensor_scalar(hT[:, s, c, :], h_ps[s][1][:, c - FA, :], w1c[:, s, F + c:F + c + 1], 0.0,
                                            ALU.add, ALU.max)
                last.then_inc(h_dve_ok, 1)

            def take_meta(j, s, value):
                dve.wait_ge(xg_in[s], value)
                v_.tensor_copy(meta_g[:, bass.ds(j, 1)], xg[:, s, GATE:GATE + 1])
                v_.tensor_copy(meta_d[:, bass.ds(j, 1)], xg[:, s, DEST:DEST + 1]).then_inc(meta_ok, 1)

            def add_constant(j, s):
                dve.wait_ge(y_t, j + 1)
                if not isinstance(j, int) or j >= U:
                    dve.wait_ge(y_ok, j - U + 1)
                v_.tensor_tensor(yd[:, s, :], y_ps[:, s, :], w1c[:, s, F + FC:WX], ALU.add).then_inc(yd_ok, 1)

            dve.wait_ge(W1_in, 16)
            dve.wait_ge(w1b_ok, 1)
            dve.wait_ge(d_ok, 1)
            experts = table_values(expert_i, 0, mybir.EngineType.DVE, E - 1)
            take_w1(0, 0, experts[0])
            take_w1(1, 1, experts[1])
            take_meta(0, 0, 16)
            take_meta(1, 1, 16)
            relu_part(0, 0)

            def expert_step(j, s, it, ahead2, ahead1, e):
                if ahead2:
                    take_w1(j + 2, (s + 2) % U, e)
                    loads = (s + 2) // U + 1
                    take_meta(j + 2, (s + 2) % U, 16 * loads if it is None else 16 * it + 16 * loads)
                if ahead1:
                    relu_part(j + 1, (s + 1) % U)
                add_constant(j, s)

            experts = table_values(expert_i, 2, mybir.EngineType.DVE, E - 1)
            for s in range(U):
                expert_step(s, s, None, True, True, experts[s])
            with dve.Fori(1, IT - 1) as it:
                experts = table_values(expert_i, U * it + 2, mybir.EngineType.DVE, E - 1)
                for s in range(U):
                    expert_step(U * it + s, s, it, True, True, experts[s])
            experts = table_values(expert_i, MAXBLK - U, mybir.EngineType.DVE, E - 1)
            for s in range(U):
                expert_step(U * (IT - 1) + s, s, IT - 1, s + 2 < U, s + 1 < U, experts[U - 1])

            for b in range(B):
                ts = slice(TB * b, TB * b + TB)
                dve.wait_ge(yk_in[b], 32)
                if b in POOL_SUMS:
                    dve.wait_ge(psum_ok, POOL_SUMS.index(b) + 1)
                else:
                    v_.tensor_tensor(acc[:, ts, :], acc[:, ts, :], yk[:, 0, ts, :], ALU.add).then_inc(sum_ok, 1)
                    dve.wait_ge(sum_ok, b + 1)
                v_.tensor_tensor(acc[:, ts, :], acc[:, ts, :], yk[:, 1, ts, :], ALU.add).then_inc(out_ok, 1)

        @block.scalar
        def _(act):
            a_ = nc.scalar
            act.wait_ge(one_ok, 1)
            a_.activation(warm[:, :], one_row[:, 0:1], ACT.Exp)
            for i, src in enumerate((nm_b1, nm_b2, q_b, k_b, gamma, beta)):
                act.dma_start(rows[NB1 + i:NB1 + i + 1, :], src.unsqueeze(0)).then_inc(rows_in, 16)

            def xn_turned(b):
                act.wait_ge(xT_t, b + 1)
                a_.activation(xnT[:, b % 2, :], xT_ps.rearrange("p t c -> p (t c)"), ACT.Copy).then_inc(xnT_ok, 1)

            def normed(b):
                act.wait_ge(nmr_ok, b + 1)
                act.wait_ge(xn_ok, b + 1)
                for t in range(TB * b, TB * b + TB):
                    last = a_.activation(zrow[:, t, :, 0:H], xn[:, t, :].unsqueeze(1).to_broadcast([P, K, H]),
                                         ACT.Identity, bias=nmr[:, t:t + 1], scale=rstd[:, 1, t:t + 1])
                last.then_inc(z_ok, 1)

            def hidden(b):
                act.wait_ge(h1_t, b + 1)
                a_.activation(h1T[:, b % 2, HALF:HALF + S], h1_ps[:, :], ACT.Relu,
                              bias=cols[:, NB1:NB1 + 1]).then_inc(h1_ok, 1)

            xn_turned(0)
            act.wait_ge(cols_t, 1)
            a_.activation(cols[:, :], cols_ps, ACT.Copy).then_inc(cols_ok, 1)
            act.wait_ge(w2T_t, 1)
            a_.activation(w2T[:, :], w2T_ps, ACT.Copy).then_inc(w2T_ok, 1)
            act.wait_ge(cols_ok, 1)
            a_.activation(rb1[:, :], cols[:, 0:E * FC], ACT.Relu).then_inc(cols_ok, 1)
            act.wait_ge(free_zero, 1)
            hidden(0)
            normed(0)
            act.wait_ge(fold_t, 1)
            a_.activation(fold[:, :, :], fold_ps, ACT.Copy).then_inc(fold_ok, 1)
            act.wait_ge(kqb_t, 1)
            a_.activation(kqb[:, 0:1], kqb_ps[:, 0:1], ACT.Identity, bias=cols[:, KB:KB + 1])
            a_.activation(kqb[:, 1:2], kqb_ps[:, 1:2], ACT.Identity, bias=cols[:, QB:QB + 1]).then_inc(kqb_ok, 1)
            act.wait_ge(kqb_ok, 1)
            a_.activation(qbs[:, :], kqb[:, 1:2], ACT.Copy, scale=SCALE).then_inc(kqb_ok, 1)
            act.wait_ge(kqb_ok, 2)
            def exps(b):
                for h in range(2):
                    act.wait_ge(nmax_ok, 2 * b + h + 1)
                    for i in (2 * h, 2 * h + 1):
                        last = a_.activation(prob[:, b % 2, i, :], s_ps[h][:, i % 2, 0:WIN], ACT.Exp,
                                             bias=nmax[:, b % 2, i:i + 1], accum_out=psums[:, b % 2, i:i + 1])
                    last.then_inc(prob_ok, 1)

            def probs_turned(b):
                act.wait_ge(pT_t, b + 1)
                a_.activation(pTa[:, :, :], pTa_ps, ACT.Copy).then_inc(pTa_ok, 1)

            def second_normed(b):
                act.wait_ge(zT_t, b + 1)
                a_.activation(xn2T[:, b % 2, :], zT_ps.rearrange("p t c -> p (t c)"), ACT.Identity,
                              bias=cols[:, BE:BE + 1], scale=cols[:, GA:GA + 1]).then_inc(xn2T_ok, 1)

            def exps_routing(b):
                act.wait_ge(rel_ok, b + 1)
                a_.activation(erel[:, TB * b:TB * b + TB, :], rel[:, TB * b:TB * b + TB, :], ACT.Exp).then_inc(erel_ok, 1)

            second_normed(0)
            normed(1)
            exps_routing(0)
            for b in range(B):
                if b + 1 < B:
                    second_normed(b + 1)
                if b >= 1:
                    exps(b - 1)
                act.wait_ge(k_t, b + 1)
                a_.activation(kT[:, b, HALF:HALF + S], k_ps[:, :], ACT.Identity, bias=kqb[:, 0:1]).then_inc(k_ok, 1)
                act.wait_ge(v_t, b + 1)
                a_.activation(v[:, b, 0:TB, :], pv_ps, ACT.Copy)
                a_.activation(v[:, b, TB, :], v4_ps, ACT.Copy).then_inc(v_ok, 1)
                if b + 1 < B:
                    exps_routing(b + 1)
                act.wait_ge(q_t, b + 1)
                a_.activation(qT[:, b, :], q_ps[:, :], ACT.Identity, bias=qbs[:, 0:1], scale=SCALE).then_inc(q_ok, 1)
                if b < E // TB:
                    act.wait_ge(c_t, b + 1)
                    a_.activation(cw[:, TB * b:TB * b + TB, :], cw_ps, ACT.Copy).then_inc(c_ok, 1)
                if b >= 1:
                    probs_turned(b - 1)
                if b + 1 < B:
                    xn_turned(b + 1)
                    hidden(b + 1)
                if b + 2 < B:
                    normed(b + 2)
            exps(B - 1)
            act.wait_ge(W1_in, 16)
            a_.activation(W1x[:, :, F:F + FC], cols[:, 0:E * FC].rearrange("p (e c) -> p e c", c=FC),
                          ACT.Copy).then_inc(w1b_ok, 1)
            probs_turned(B - 1)

            def turn_block(j, s):
                act.wait_ge(xgT_t, j + 1)
                a_.activation(xgT[:, s, :], xgT_ps[:, s, :], ACT.Identity,
                              bias=cols[:, BE:BE + 1], scale=cols[:, GA:GA + 1]).then_inc(xgT_ok, 1)

            def relu_part(j, s):
                act.wait_ge(h_t0, j + 1)
                for c in range(FA):
                    last = a_.activation(hT[:, s, c, :], h_ps[s][0][:, c, :], ACT.Relu, bias=w1c[:, s, F + c:F + c + 1])
                last.then_inc(h_act_ok, 1)

            def weigh(j, s):
                act.wait_ge(yd_ok, j + 1)
                act.wait_ge(meta_ok, j + 1)
                a_.activation(ys[:, bass.ds(j, 1), :].rearrange("p o h -> p (o h)"), yd[:, s, :], ACT.Copy, scale=meta_g[:, bass.ds(j, 1)]).then_inc(y_ok, 1)

            turn_block(0, 0)
            turn_block(1, 1)
            relu_part(0, 0)

            def expert_step(j, s, ahead2, ahead1, behind1):
                if ahead2:
                    turn_block(j + 2, (s + 2) % U)
                if ahead1:
                    relu_part(j + 1, (s + 1) % U)
                if behind1:
                    weigh(j - 1, (s - 1) % U)

            for s in range(U):
                expert_step(s, s, True, True, s >= 1)
            with act.Fori(1, IT - 1) as it:
                for s in range(U):
                    expert_step(U * it + s, s, True, True, True)
            for s in range(U):
                expert_step(U * (IT - 1) + s, s, s + 2 < U, s + 1 < U, True)
            weigh(MAXBLK - 1, U - 1)

            act.wait_ge(y_out, 16 * MAXBLK)
            for b in range(1, B, 2):
                act.dma_start(yk[:, 0, TB * b:TB * b + TB, :], yt[:, 0, TB * b:TB * b + TB, :]).then_inc(yk_in[b], 16)
                act.dma_start(yk[:, 1, TB * b:TB * b + TB, :], yt[:, 1, TB * b:TB * b + TB, :]).then_inc(yk_in[b], 16)

        @block.tensor
        def _(pe):
            t_ = nc.tensor

            def turn_xn(b):
                pe.wait_ge(xn_ok, b + 1)
                for i in range(TB):
                    last = t_.transpose(xT_ps[:, i, :], xn[:, TB * b + i, :], ident[:, :])
                last.then_inc(xT_t, 1)

            def hidden(b):
                pe.wait_ge(xnT_ok, b + 1)
                if b >= 1:
                    pe.wait_ge(k_ok, b)
                t_.matmul(h1_ps[:, :], w1_sb[:, :], xnT[:, b % 2, :], start=True, stop=True).then_inc(h1_t, 1)

            pe.wait_ge(ident_ok, 1)
            turn_xn(0)
            pe.wait_ge(rows_in, 16 * 6)
            pe.wait_ge(b_in, 16 * 2)
            t_.transpose(cols_ps, rows[:, :], ident[0:NROWS, 0:NROWS]).then_inc(cols_t, 1)
            pe.wait_ge(w2_in, 16)
            t_.transpose(w2T_ps, w2_sb[:, :], ident[:, :]).then_inc(w2T_t, 1)
            pe.wait_ge(w1_in, 16)
            hidden(0)
            pe.wait_ge(w2T_ok, 1)
            pe.wait_ge(wa_in, 48)
            t_.matmul(fold_ps, w2T[:, :], wkqv[:, :, :], start=True, stop=True).then_inc(fold_t, 1)
            pe.wait_ge(cols_ok, 2)
            pe.wait_ge(free_zero, 1)
            for i in range(2):
                t_.matmul(kqb_ps[:, i:i + 1], wkqv[:, i, :], cols[:, NB2:NB2 + 1], start=True, stop=True)
            t_.matmul(vb_ps, cols[:, NB2:NB2 + 1].to_broadcast([H, P]), wkqv[:, 2, :],
                      start=True, stop=True)
            t_.matmul(b2_ps, ones_e[B2:B2 + E, :], rows[B2:B2 + E, :], start=True, stop=True).then_inc(kqb_t, 1)
            pe.wait_ge(wr_in, 16)

            def constant_row(e):
                for c in range(FC):
                    last = t_.matmul(cw_ps[:, e % TB, :], rb1[:, e * FC + c:e * FC + c + 1].to_broadcast([P, P]),
                                     W2s[:, e, c, :], start=(c == 0), stop=(c == FC - 1))
                if e % TB == TB - 1:
                    last.then_inc(c_t, 1)

            def scores(b):
                pe.wait_ge(q_ok, b + 1)
                for h in range(2):
                    if b >= 1:
                        pe.wait_ge(prob_ok, 2 * b - 1 + h)
                    for i in (2 * h, 2 * h + 1):
                        t_.matmul(s_ps[h][:, i % 2, 0:WIN], qT[:, b, i * P:(i + 1) * P],
                                  kT[:, b, i * P:i * P + WIN], start=True, stop=False)
                        last = t_.matmul(s_ps[h][:, i % 2, 0:WIN], identb[:, :], band[:, i, :], start=False, stop=True)
                    last.then_inc(s_t, 1)

            def turn_probs(b):
                pe.wait_ge(prob_ok, 2 * b + 2)
                if b >= 1:
                    pe.wait_ge(pTa_ok, b)
                else:
                    pe.wait_ge(c_ok, E // TB)
                for i in range(TB):
                    t_.transpose(pTa_ps[:, i, :], prob[:, b % 2, i, 0:P], ident[:, :])
                    last = t_.transpose(pTb_ps[0:CH, i, :], prob[:, b % 2, i, P:WIN], ident[:, :])
                last.then_inc(pT_t, 1)

            def attend(b):
                pe.wait_ge(pTa_ok, b + 1)
                pe.wait_ge(pTb_ok, b + 1)
                for i in range(TB):
                    t_.matmul(pv_ps[:, i, :], pTa[:, i, :], v[:, b, i, :], start=True, stop=False)
                    last = t_.matmul(pv_ps[:, i, :], pTb[:, i, :], v[0:CH, b, i + 1, :], start=False, stop=True)
                last.then_inc(pv_t, 1)

            def turn_z(b):
                pe.wait_ge(z_ok, b + 1)
                pe.wait_ge(xnT_ok, max(b, 1))
                for i in range(TB):
                    last = t_.transpose(zT_ps[:, i, :], zrow[:, TB * b + i, 0, 0:H], ident[:, :])
                last.then_inc(zT_t, 1)

            def logits(b):
                pe.wait_ge(xn2T_ok, b + 1)
                if b >= 1:
                    pe.wait_ge(slot_ok, b)
                for i in range(TB):
                    last = t_.matmul(logit_ps[:, TB * b + i, :], xn2T[:, b % 2, i * P:(i + 1) * P], wr_sb[:, :],
                                     start=True, stop=True)
                last.then_inc(logit_t, 1)

            def ranks(b):
                pe.wait_ge(mask_ok, b + 1)
                r = rank_ps[:, TB * b:TB * b + TB, :]
                t_.matmul(r, upper[:, :], mask[:, TB * b:TB * b + TB, :], start=True, stop=False, skip_group_check=True)
                for i in range(TB - 1):
                    t_.matmul(rank_ps[:, TB * b + i + 1:TB * b + TB, :], ones[:, :],
                              mask[:, TB * b + i:TB * b + i + 1, :].to_broadcast([P, TB - 1 - i, E]),
                              start=False, stop=False, skip_group_check=True)
                if b >= 1:
                    pe.wait_ge(before_ok, b)
                t_.matmul(r, ones[:, :], before[:, b:b + 1, :].to_broadcast([P, TB, E]),
                          start=False, stop=True, skip_group_check=True).then_inc(rank_t, 1)

            turn_z(0)
            logits(0)
            for b in range(B):
                if b + 1 < B:
                    turn_z(b + 1)
                pe.wait_ge(h1_ok, b + 1)
                if b == 0:
                    pe.wait_ge(fold_ok, 1)
                t_.matmul(k_ps[:, :], fold[:, 0, :], h1T[:, b % 2, HALF:HALF + S], start=True, stop=True).then_inc(k_t, 1)
                if b == 0:
                    pe.wait_ge(vb_ok, 1)
                if b >= 2:
                    pe.wait_ge(acc_ok, b - 1)
                    pe.wait_ge(pTb_ok, b - 1)
                for i in range(TB + 1):
                    last = t_.matmul(pv_ps[:, i, :] if i < TB else v4_ps, h1T[:, b % 2, i * P:(i + 1) * P],
                                     fold[:, 2, :], start=True, stop=True)
                last.then_inc(v_t, 1)
                if b == 0:
                    pe.wait_ge(free_zero, 1)
                    pe.wait_ge(routing_consts, 1)
                    ranks(0)
                if b + 1 < B:
                    logits(b + 1)
                else:
                    pe.wait_ge(xn2T_ok, B)
                t_.matmul(q_ps[:, :], fold[:, 1, :], h1T[:, b % 2, HALF:HALF + S], start=True, stop=True).then_inc(q_t, 1)
                if b >= 1:
                    pe.wait_ge(v_ok, b + 1)
                    turn_probs(b - 1)
                if b == 0:
                    pe.wait_ge(W2_in, 16)
                    for e in range(TB):
                        constant_row(e)
                if b + 1 < B:
                    ranks(b + 1)
                if b + 1 < B:
                    pe.wait_ge(q_ok, b + 1)
                    turn_xn(b + 1)
                if b >= 1:
                    attend(b - 1)
                if b + 1 < B:
                    hidden(b + 1)
                if b == 0:
                    pe.wait_ge(consts, 1)
                scores(b)
                if b == B - 2:
                    pe.wait_ge(before_ok, B)
                    pe.wait_ge(slot_ok, B)
                    t_.matmul(total_ps, ones[:, :], before[:, B, :], start=True, stop=True).then_inc(total_t, 1)
                if b == 0:
                    pe.wait_ge(c_ok, 1)
                    for e in range(TB, 2 * TB):
                        constant_row(e)

            pe.wait_ge(acc_ok, B - 1)
            turn_probs(B - 1)
            attend(B - 1)

            def turn_block(j, s, value):
                pe.wait_ge(xg_in[s], value)
                if not isinstance(j, int) or j >= 1:
                    pe.wait_ge(xgT_ok, j)
                t_.transpose(xgT_ps[:, s, :], xg[:, s, 0:H], ident[:, :]).then_inc(xgT_t, 1)

            def first(j, s, turned):
                if not turned:
                    pe.wait_ge(xgT_ok, j + 1)
                pe.wait_ge(w1c_ok, j + 1)
                for half, done in enumerate((h_t0, h_t1)):
                    for f in range(FA * half, FC if half else FA):
                        last = t_.matmul(h_ps[s][half][:, f - FA * half, :], w1c[:, s, f * P:(f + 1) * P], xgT[:, s, :],
                                         start=True, stop=True)
                    last.then_inc(done, 1)

            def second(j, s, e):
                pe.wait_ge(h_act_ok, j + 1)
                pe.wait_ge(h_dve_ok, j + 1)
                if not isinstance(j, int) or j >= 1:
                    pe.wait_ge(yd_ok, j)
                for c in range(FC):
                    last = t_.matmul(y_ps[:, s, :], hT[:, s, c, :],
                                     W2s[:, bass.ds(e, 1), c, :].rearrange("p o h -> p (o h)"),
                                     start=(c == 0), stop=(c == FC - 1))
                last.then_inc(y_t, 1)

            pe.wait_ge(table_ok, 1)
            turn_block(0, 0, 16)
            turn_block(1, 1, 16)
            first(0, 0, True)
            pe.wait_ge(acc_ok, B)
            pe.wait_ge(c_ok, E // TB)

            def ahead(it, s, ahead2, ahead1):
                j = U * it + s
                if ahead2:
                    turn_block(j + 2, (s + 2) % U, 16 * it + 16 * ((s + 2) // U) + 16)
                if ahead1:
                    first(j + 1, (s + 1) % U, ahead2)

            def expert_steps(it, last):
                ahead(it, 0, True, True)
                experts = table_values(expert_i, U * it, mybir.EngineType.PE, E - 1)
                second(U * it, 0, experts[0])
                for s in range(1, U):
                    ahead(it, s, s + 2 < U or not last, s + 1 < U or not last)
                    second(U * it + s, s, experts[s])

            with pe.Fori(0, IT - 1) as it:
                expert_steps(it, False)
            expert_steps(IT - 1, True)


_INS = ['L0_attn_x', 'L0_attn_nm_w1', 'L0_attn_nm_b1', 'L0_attn_nm_w2', 'L0_attn_nm_b2', 'L0_attn_q_w',
        'L0_attn_q_b', 'L0_attn_k_w', 'L0_attn_k_b', 'L0_attn_v_w', 'L0_attn_v_b', 'L0_ffn_gamma', 'L0_ffn_beta',
        'L0_ffn_Wr', 'L0_ffn_br', 'L0_ffn_W1', 'L0_ffn_b1', 'L0_ffn_W2', 'L0_ffn_b2']
_OUTS = [((4, 512, 128), 'float32')]


def kernel(**inputs):
    import numpy as _np
    import concourse.bacc as _bacc
    from concourse import mybir as _mybir
    from concourse.bass_utils import run_bass_kernel_spmd as _run

    nc = _bacc.Bacc("TRN2", target_bir_lowering=False, num_devices=1)
    arrays, args = {}, []
    for name in _INS:
        a = _np.ascontiguousarray(inputs[name])
        arrays[f"in_{name}_dram"] = a
        args.append(nc.dram_tensor(f"in_{name}_dram", a.shape, _mybir.dt.from_np(a.dtype), kind="ExternalInput").ap())
    for i, (shape, dtype) in enumerate(_OUTS):
        dt = _mybir.dt.from_np(_np.dtype(dtype))
        args.append(nc.dram_tensor(f"out_{i}_dram", shape, dt, kind="ExternalOutput").ap())
    build(nc, *args)
    r = _run(nc, [arrays], core_ids=[0])
    return r.results[0]["out_0_dram"]
```

```python
import concourse.bass as bass
from concourse import mybir
from contextlib import ExitStack


def build(nc, x, nm_w1, nm_b1, nm_w2, nm_b2, q_w, q_b, k_w, k_b, v_w, v_b,
          gamma, beta, Wr, br, W1, b1, W2, b2, out):
    f32 = mybir.dt.float32
    i32 = mybir.dt.int32
    u32 = mybir.dt.uint32
    bf16 = mybir.dt.bfloat16
    ALU = mybir.AluOpType
    ACT = mybir.ActivationFunctionType
    AX = mybir.AxisListType.X

    P = 128
    B, S, H = x.shape
    E, _, F = W1.shape
    K = 2
    N = B * S
    TB = S // P
    NT = N // P
    FC = F // P
    HALF = 32
    WIN = P + 2 * HALF
    CH = WIN - P
    PADK = (TB + 1) * P
    EPS = 1e-5
    SCALE = float(H) ** -0.5
    NEG = -1e30
    ROW = H + 2
    GATE, DEST = H, H + 1
    REG = N + P
    MAXBLK = (N * K - E) // P + E
    NOWHERE = 1 << 20
    U = 3
    IT = MAXBLK // U
    WX = F + FC + H
    WARMUP = 40
    FA = 3
    OUT_PARTS = [slice(TB * b, TB * b + TB) for b in range(B - 1)] + [
        slice(NT - TB, NT - TB // 2), slice(NT - TB // 2, NT)]
    assert H == P and TB == 4 and E % TB == 0 and MAXBLK == U * IT and N * K // P >= E

    xt = x.rearrange("b (t p) h -> p (b t) h", p=P)
    ot = out.rearrange("b (t p) h -> p (b t) h", p=P)
    disp = nc.dram_tensor("disp", [E * REG + P, ROW], f32, kind="Internal").ap()
    ysel = nc.dram_tensor("ysel", [K * N, H], f32, kind="Internal").ap()
    yt = ysel.rearrange("(k t p) h -> p k t h", k=K, p=P)

    ctx = ExitStack()
    with ctx:
        def sb(name, shape, dt=f32):
            return ctx.enter_context(nc.sbuf_tensor(name, shape, dt))

        def sem(name):
            return ctx.enter_context(nc.semaphore(name))

        ident = sb("ident", [P, P])
        upper = sb("upper", [P, P], bf16)
        ones = sb("ones", [P, P], bf16)
        ones_e = sb("ones_e", [P, P])
        minus_half = sb("minus_half", [P, TB])
        identb = sb("identb", [P, P], bf16)
        band = sb("band", [P, TB, WIN], bf16)
        iota_e = sb("iota_e", [P, E])
        region = sb("region", [P, E])
        iota_j = sb("iota_j", [1, MAXBLK])
        iota_128 = sb("iota_128", [1, NT])
        one_row = sb("one_row", [1, E])
        warm = sb("warm", [1, 1])
        padrow = sb("padrow", [P, ROW])
        w1_sb = sb("w1_sb", [H, H])
        w2_sb = sb("w2_sb", [H, H])
        wkqv = sb("wkqv", [H, 3, H])
        w2T = sb("w2T", [H, H])
        fold = sb("fold", [H, 3, H])
        wr_sb = sb("wr_sb", [H, E])
        wg = sb("wg", [H, E])
        wg_sum = sb("wg_sum", [P, E])
        br_bc = sb("br_bc", [P, E])
        vb_bc = sb("vb_bc", [P, H])
        NROWS = E * FC + E + 6
        B2, NB1, NB2, QB, KB, GA, BE = E * FC, E * FC + E, NROWS - 5, NROWS - 4, NROWS - 3, NROWS - 2, NROWS - 1
        rows = sb("rows", [NROWS, H])
        cols = sb("cols", [P, NROWS])
        kqb = sb("kqb", [P, 2])
        qbs = sb("qbs", [P, 1])
        W1x = sb("W1x", [H, E, WX])
        W2s = sb("W2s", [P, E, FC, H])
        x_sb = sb("x_sb", [P, NT, H])
        xn = sb("xn", [P, NT, H])
        stats = sb("stats", [P, 2, NT, 6])
        mv = sb("mv", [P, 2, NT, 2])
        veps = sb("veps", [P, 2, NT])
        rstd = sb("rstd", [P, 2, NT])
        negmean = sb("negmean", [P, NT])
        nmr = sb("nmr", [P, NT])
        zrow = sb("zrow", [P, NT, K, ROW])
        shift = sb("shift", [P, NT, E])
        scaled = sb("scaled", [P, NT, E])
        lg = sb("lg", [P, NT, E])
        best = sb("best", [P, NT, 8])
        bidx = sb("bidx", [P, NT, 8], u32)
        bidxf = sb("bidxf", [P, NT, K])
        rel = sb("rel", [P, NT, E])
        erel = sb("erel", [P, NT, E])
        esum = sb("esum", [P, NT])
        einv = sb("einv", [P, NT])
        oh = sb("oh", [P, NT, K, E])
        mask = sb("mask", [P, NT, E], bf16)
        msum = sb("msum", [P, B, E], bf16)
        before = sb("before", [P, B + 1, E], bf16)
        slot = sb("slot", [P, NT, E])
        ohslot = sb("ohslot", [P, NT, K, E])
        pos = sb("pos", [P, NT, K], i32)
        over = sb("over", [1, E, NT])
        nblk = sb("nblk", [1, E])
        count_i = sb("count_i", [1, E], i32)
        incl = sb("incl", [1, E])
        past = sb("past", [1, MAXBLK, E])
        pastn = sb("pastn", [1, MAXBLK, E])
        eb = sb("eb", [1, MAXBLK])
        excl = sb("excl", [1, MAXBLK])
        jrel = sb("jrel", [1, MAXBLK])
        startf = sb("startf", [1, MAXBLK])
        start_i = sb("start_i", [1, MAXBLK], i32)
        expert_i = sb("expert_i", [1, MAXBLK], i32)
        xnT = sb("xnT", [H, 3, S])
        h1T = sb("h1T", [H, 2, PADK])
        qT = sb("qT", [H, B, S])
        kT = sb("kT", [H, B, PADK])
        v = sb("v", [P, B, TB + 1, H])
        nmax = sb("nmax", [P, 2, TB])
        prob = sb("prob", [P, 2, TB, WIN])
        psums = sb("psums", [P, 2, TB])
        pinv = sb("pinv", [P, 2, TB])
        pTa = sb("pTa", [P, TB, P])
        pTb = sb("pTb", [CH, TB, P])
        acc = sb("acc", [P, NT, H])
        rb1 = sb("rb1", [P, E * FC])
        cw = sb("cw", [P, E, H])
        b2_sum = sb("b2_sum", [P, H])
        c_tot = sb("c_tot", [P, H])
        xg = sb("xg", [P, U, ROW])
        meta_g = sb("meta_g", [P, MAXBLK])
        meta_d = sb("meta_d", [P, MAXBLK], i32)
        yd = sb("yd", [P, U, H])
        xgT = sb("xgT", [H, U, P])
        w1c = sb("w1c", [H, U, WX])
        hT = sb("hT", [P, U, FC, P])
        ys = sb("ys", [P, MAXBLK, H])
        yk = sb("yk", [P, K, NT, H])

        bank = [ctx.enter_context(nc.psum_tensor(f"bank{i}", [P, 512], f32)) for i in range(8)]

        def tiles(i):
            return bank[i][:, :].rearrange("p (t c) -> p t c", t=TB)

        s_ps = [bank[i][:, :].rearrange("p (t c) -> p t c", t=2) for i in (0, 1)]
        h1_ps, k_ps = bank[2], bank[2]
        xT_ps, q_ps = [tiles(i) for i in (3, 0, 3, 3)], bank[3]
        logit_ps = bank[4][:, 0:NT * E].rearrange("p (t e) -> p t e", e=E)
        rank_ps = bank[4][:, NT * E:2 * NT * E].rearrange("p (t e) -> p t e", e=E)
        total_ps = bank[4][:, 2 * NT * E:2 * NT * E + E]
        pv_ps, v4_ps = tiles(5), bank[6][:, 0:H]
        pTa_ps, pTb_ps = tiles(7), tiles(6)
        cw_ps = tiles(7)
        fold_ps = bank[0][:, 0:3 * H].rearrange("p (a c) -> p a c", a=3)
        kqb_ps = bank[1][:, 0:2]
        w2T_ps = bank[5][:, 0:H]
        vb_ps, b2_ps = bank[6][:, 0:H], bank[6][:, H:2 * H]
        sums_ps = bank[7][:, 2 * H:2 * H + 2 * E].rearrange("p (a e) -> p a e", a=2)
        cols_ps = bank[7][:, 0:NROWS]
        h_ps = [[tiles(i) for i in pair] for pair in ((0, 1), (2, 4), (5, 6))]
        xgT_ps, xgT0_ps = tiles(3), tiles(4)
        y_ps = tiles(7)

        x_in = [sem(f"x_in{b}") for b in range(B)]
        rows_in = sem("rows_in")
        b_in = sem("b_in")
        w1_in = sem("w1_in")
        w2_in = sem("w2_in")
        wr_in = sem("wr_in")
        br_in = sem("br_in")
        wa_in = sem("wa_in")
        vb_in = sem("vb_in")
        W1_in = sem("W1_in")
        W2_in = sem("W2_in")
        pads_out = sem("pads_out")
        sent = sem("sent")
        xg_in = [sem(f"xg_in{s}") for s in range(U)]
        y_out = sem("y_out")
        yk_in = [[sem(f"yk_in{k}_{b}") for b in range(B)] for k in range(K)]
        stored = sem("stored")
        (consts, routing_consts, ident_ok, cols_t, cols_ok, stat1, var1, rstd1, xn_ok, stat2, var2, rstd2, nmr_ok, z_ok,
         wg_ok, xT_t, xnT_ok, shift_ok, logit_t, scaled_ok, lg_ok, best_ok, rel_ok, erel_ok, esum_ok, einv_ok, gate_ok,
         idx_ok, idxf_ok, oh_ok, mask_ok, msum_ok, before_ok, rank_t, slot_ok, ohslot_ok, pos_ok,
         sums_t, sums_ok, w2T_t, w2T_ok, fold_t, fold_ok, kqb_t, kqb_ok, vb_ok, h1_t, h1_ok, k_t, k_ok, q_t, q_ok, v_t, v_ok,
         total_t, table, counts_ok, table_ok, s_t, nmax_ok, prob_ok, pT_t, pTa_ok, pTb_ok, pinv_ok,
         pv_t, acc_ok, res_ok, c_t, c_ok, cstep, d_ok,
         xgT_t, xgT_ok, meta_ok, w1b_ok, w1c_ok, h_t0, h_t1, h_act_ok, h_dve_ok, y_t, yd_ok, y_ok, sum_ok, out_ok,
         const_step, free_zero, one_ok) = [sem(n) for n in (
             "consts routing_consts ident_ok cols_t cols_ok stat1 var1 rstd1 xn_ok stat2 var2 rstd2 nmr_ok z_ok "
             "wg_ok xT_t xnT_ok shift_ok logit_t scaled_ok lg_ok best_ok rel_ok erel_ok esum_ok einv_ok gate_ok "
             "idx_ok idxf_ok oh_ok mask_ok msum_ok before_ok rank_t slot_ok ohslot_ok pos_ok "
             "sums_t sums_ok w2T_t w2T_ok fold_t fold_ok kqb_t kqb_ok vb_ok h1_t h1_ok k_t k_ok q_t q_ok v_t v_ok "
             "total_t table counts_ok table_ok s_t nmax_ok prob_ok pT_t pTa_ok pTb_ok pinv_ok "
             "pv_t acc_ok res_ok c_t c_ok cstep d_ok "
             "xgT_t xgT_ok meta_ok w1b_ok w1c_ok h_t0 h_t1 h_act_ok h_dve_ok y_t yd_ok y_ok sum_ok out_ok "
             "const_step free_zero one_ok").split()]

        block = ctx.enter_context(nc.Block())

        def table_values(table_row, j, engine, top, count=U):
            return nc.values_load_multi_w_load_instructions(
                table_row[0:1, bass.ds(j, count)], engines=[engine], min_val=0, max_val=top,
                skip_runtime_bounds_check_because="starts and experts are clamped to top; a count is at most N")[1]

        @block.sync
        def _(sp):
            def load_x(b):
                sp.dma_start(x_sb[:, TB * b:TB * b + TB, :], xt[:, TB * b:TB * b + TB, :]).then_inc(x_in[b], 16)

            load_x(0)
            sp.dma_start(w1_sb[:, :], nm_w1).then_inc(w1_in, 16)
            sp.dma_start(wr_sb[:, :], Wr).then_inc(wr_in, 16)
            load_x(1)
            sp.dma_start(w2_sb[:, :], nm_w2).then_inc(w2_in, 16)
            for i, w in enumerate((k_w, q_w, v_w)):
                sp.dma_start(wkqv[:, i, :], w).then_inc(wa_in, 16)
            sp.dma_start(br_bc[:, :], br.partition_broadcast(P)).then_inc(br_in, 16)
            load_x(2)
            sp.dma_start(vb_bc[:, :], v_b.partition_broadcast(P)).then_inc(vb_in, 16)
            sp.dma_start(W2s[:, :, :, :], W2.rearrange("e (c p) h -> p e c h", p=P)).then_inc(W2_in, 16)
            load_x(3)
            sp.dma_start(W1x[:, :, 0:F], W1.rearrange("e h f -> h e f")).then_inc(W1_in, 16)
            sp.wait_ge(routing_consts, 1)
            sp.dma_start(disp[E * REG:E * REG + P, :], padrow[:, :]).then_inc(pads_out, 16)
            sp.wait_ge(counts_ok, 1)
            counts = [n for e in (0, E // 2) for n in table_values(count_i, e, mybir.EngineType.SP, N, E // 2)]
            for e in range(E):
                sp.dma_start(disp[bass.ds(counts[e] + e * REG, P), :], padrow[:, :]).then_inc(pads_out, 16)
            sp.wait_ge(pads_out, 16 * (E + 1))
            sp.wait_ge(sent, 16 * NT * K)

            def load_block(r, s):
                sp.dma_start(xg[:, s, :], disp[bass.ds(r, P), :]).then_inc(xg_in[s], 16)

            sp.wait_ge(table_ok, 1)
            starts = table_values(start_i, 0, mybir.EngineType.SP, E * REG)
            for s in range(U):
                load_block(starts[s], s)
            with sp.Fori(1, IT) as it:
                starts = table_values(start_i, U * it, mybir.EngineType.SP, E * REG)
                for s in range(U):
                    sp.wait_ge(xgT_t, U * it - U + s + 1)
                    sp.wait_ge(meta_ok, U * it - U + s + 1)
                    load_block(starts[s], s)

            sp.wait_ge(y_out, 16 * MAXBLK)
            for k in range(K):
                for b in range(0, B, 2):
                    ts = slice(TB * b, TB * b + TB)
                    sp.dma_start(yk[:, k, ts, :], yt[:, k, ts, :]).then_inc(yk_in[k][b], 16)
            for i, ts in enumerate(OUT_PARTS):
                sp.wait_ge(out_ok, i + 1)
                sp.dma_start(ot[:, ts, :], acc[:, ts, :]).then_inc(stored, 16)
            sp.wait_ge(stored, 16 * len(OUT_PARTS))

        @block.gpsimd
        def _(pool):
            g = nc.gpsimd
            g.memset(ident[:, :], 0.0)
            g.memset(minus_half[:, :], -0.5).then_inc(const_step, 1)
            pool.wait_ge(const_step, 1)
            g.affine_select(out=ident[:, :], in_=ident[:, :], compare_op=ALU.not_equal, fill=1.0,
                            base=0, pattern=[[-1, P]], channel_multiplier=1).then_inc(ident_ok, 1)

            g.dma_start(rows[0:B2, :], b1.rearrange("e (c p) -> (e c) p", p=P)).then_inc(b_in, 16)
            g.dma_start(rows[B2:B2 + E, :], b2).then_inc(b_in, 16)

            g.memset(identb[:, :], 0.0)
            g.memset(upper[:, :], 0.0)
            g.memset(band[:, :, :], 0.0)
            g.memset(padrow[:, :], 0.0).then_inc(const_step, 1)

            def small_constants():
                g.iota(iota_e[:, :], pattern=[[1, E]], base=0, channel_multiplier=0,
                       allow_small_or_imprecise_dtypes=True)
                g.iota(region[:, :], pattern=[[REG, E]], base=0, channel_multiplier=0,
                       allow_small_or_imprecise_dtypes=True)
                g.iota(iota_j[:, :], pattern=[[1, MAXBLK]], base=0, channel_multiplier=0,
                       allow_small_or_imprecise_dtypes=True)
                g.iota(iota_128[:, :], pattern=[[P, NT]], base=0, channel_multiplier=0,
                       allow_small_or_imprecise_dtypes=True)
                g.iota(zrow[:, :, :, DEST:DEST + 1].rearrange("p t k o -> p t (k o)"),
                       pattern=[[P, NT], [N, K]], base=0, channel_multiplier=1,
                       allow_small_or_imprecise_dtypes=True)
                pool.wait_ge(const_step, 2)
                g.memset(padrow[:, DEST:DEST + 1], float(NOWHERE))
                g.affine_select(out=upper[:, :], in_=upper[:, :], compare_op=ALU.is_ge, fill=1.0,
                                base=0, pattern=[[-1, P]], channel_multiplier=1).then_inc(routing_consts, 1)

            def band_constants():
                g.affine_select(out=identb[:, :], in_=identb[:, :], compare_op=ALU.not_equal, fill=1.0,
                                base=0, pattern=[[-1, P]], channel_multiplier=1)
                g.affine_select(out=band[:, :, :], in_=band[:, :, :], compare_op=ALU.is_ge, fill=NEG,
                                base=0, pattern=[[0, TB], [1, WIN]], channel_multiplier=-1).then_inc(const_step, 1)
                pool.wait_ge(const_step, 3)
                g.affine_select(out=band[:, :, :], in_=band[:, :, :], compare_op=ALU.is_ge, fill=NEG,
                                base=2 * HALF, pattern=[[0, TB], [-1, WIN]],
                                channel_multiplier=1).then_inc(const_step, 1)
                pool.wait_ge(const_step, 4)
                g.memset(band[:, 0, 0:HALF], NEG)
                g.memset(band[:, TB - 1, HALF + P:WIN], NEG).then_inc(consts, 1)

            def inverse_root(l, b, var, done):
                pool.wait_ge(var, b + 1)
                g.tensor_tensor(rstd[:, l, TB * b:TB * b + TB], veps[:, l, TB * b:TB * b + TB],
                                minus_half[:, :], ALU.pow).then_inc(done, 1)
                if l == 1:
                    pool.wait_ge(done, b + 1)
                    g.tensor_tensor(nmr[:, TB * b:TB * b + TB], negmean[:, TB * b:TB * b + TB],
                                    rstd[:, 1, TB * b:TB * b + TB], ALU.mult).then_inc(nmr_ok, 1)

            def send(b, k, tiles_sent=range(TB)):
                for t in (TB * b + i for i in tiles_sent):
                    g.indirect_dma_start(disp[:, :], bass.IndirectOffsetOnAxis(ap=pos[:, t, k:k + 1], axis=0),
                                         zrow[:, t, k, :], None).then_inc(sent, 16)

            inverse_root(0, 0, var1, rstd1)
            small_constants()
            inverse_root(1, 0, var2, rstd2)
            inverse_root(0, 1, var1, rstd1)
            band_constants()
            inverse_root(0, 2, var1, rstd1)
            for b in range(B):
                pool.wait_ge(pos_ok, b + 1)
                pool.wait_ge(gate_ok, b + 1)
                pool.wait_ge(z_ok, b + 1)
                if b == 0:
                    send(0, 0, range(TB // 2))
                    inverse_root(1, 1, var2, rstd2)
                    send(0, 0, range(TB // 2, TB))
                else:
                    send(b, 0)
                if b == 1:
                    inverse_root(1, 3, var2, rstd2)
                send(b, 1)
                if b == 0:
                    inverse_root(0, 3, var1, rstd1)
                    inverse_root(1, 2, var2, rstd2)

            def send_back(j):
                pool.wait_ge(y_ok, j + 1)
                pool.wait_ge(meta_ok, j + 1)
                g.indirect_dma_start(ysel[:, :], bass.IndirectOffsetOnAxis(ap=meta_d[:, j:j + 1], axis=0),
                                     ys[:, j, :], None, bounds_check=K * N - 1, oob_is_err=False).then_inc(y_out, 16)

            def residual(n):
                b, what, half = n // 6, n % 6 // 2, n % 2
                ts = slice(TB * b + TB // 2 * half, TB * b + TB // 2 * half + TB // 2)
                part = (x_sb[:, ts, :], xn[:, ts, :], vb_bc[:, :].unsqueeze(1).to_broadcast([P, TB // 2, H]))[what]
                if n == 0:
                    pool.wait_ge(acc_ok, B)
                elif n >= 2:
                    pool.wait_ge(res_ok, n - 1)
                g.tensor_tensor(acc[:, ts, :], acc[:, ts, :], part, ALU.add).then_inc(res_ok, 1)

            for j in range(MAXBLK):
                send_back(j)
                if j < 6 * B:
                    residual(j)

        @block.vector
        def _(dve):
            v_ = nc.vector

            def norm1_stats(b):
                dve.wait_ge(x_in[b], 16)
                for t in range(TB * b, TB * b + TB):
                    last = v_.bn_stats(stats[:, 0, t, :], x_sb[:, t, :])
                last.then_inc(stat1, 1)
                dve.wait_ge(stat1, 2 * b + 1)
                for t in range(TB * b, TB * b + TB):
                    last = v_.bn_aggr(mv[:, 0, t, :], stats[:, 0, t, :])
                last.then_inc(stat1, 1)
                add_eps(b)

            def add_eps(b):
                dve.wait_ge(stat1, 2 * b + 2)
                v_.tensor_scalar(veps[:, 0, TB * b:TB * b + TB], mv[:, 0, TB * b:TB * b + TB, 1], EPS, None,
                                 ALU.add).then_inc(var1, 1)

            def norm1_apply(b):
                dve.wait_ge(rstd1, b + 1)
                for t in range(TB * b, TB * b + TB):
                    last = v_.tensor_scalar(xn[:, t, :], x_sb[:, t, :], mv[:, 0, t, 0:1], rstd[:, 0, t:t + 1],
                                            ALU.subtract, ALU.mult)
                last.then_inc(xn_ok, 1)

            def norm2_stats(b):
                dve.wait_ge(xn_ok, b + 1)
                for t in range(TB * b, TB * b + TB):
                    last = v_.bn_stats(stats[:, 1, t, :], xn[:, t, :])
                last.then_inc(stat2, 1)
                dve.wait_ge(stat2, 2 * b + 1)
                for t in range(TB * b, TB * b + TB):
                    last = v_.bn_aggr(mv[:, 1, t, :], stats[:, 1, t, :])
                last.then_inc(stat2, 1)
                dve.wait_ge(stat2, 2 * b + 2)
                v_.tensor_scalar(negmean[:, TB * b:TB * b + TB], mv[:, 1, TB * b:TB * b + TB, 0], -1.0, None, ALU.mult)
                v_.tensor_scalar(veps[:, 1, TB * b:TB * b + TB], mv[:, 1, TB * b:TB * b + TB, 1], EPS, None,
                                 ALU.add).then_inc(var2, 1)

            def shift_logits(b):
                ts = slice(TB * b, TB * b + TB)
                dve.wait_ge(nmr_ok, b + 1)
                v_.tensor_tensor(shift[:, ts, :], nmr[:, ts].unsqueeze(2).to_broadcast([P, TB, E]),
                                 wg_sum[:, :].unsqueeze(1).to_broadcast([P, TB, E]), ALU.mult).then_inc(shift_ok, 1)
                dve.wait_ge(shift_ok, 2 * b + 1)
                v_.tensor_tensor(shift[:, ts, :], shift[:, ts, :], br_bc[:, :].unsqueeze(1).to_broadcast([P, TB, E]),
                                 ALU.add).then_inc(shift_ok, 1)

            def choose(b):
                ts = slice(TB * b, TB * b + TB)
                beside = b + 2 if b < 2 else None

                def tile_stats(i):
                    if beside is not None:
                        t = TB * beside + i
                        ins = v_.bn_stats(stats[:, 0, t, :], x_sb[:, t, :])
                        if i == TB - 1:
                            ins.then_inc(stat1, 1)

                dve.wait_ge(logit_t, b + 1)
                v_.tensor_tensor(scaled[:, ts, :], logit_ps[:, ts, :],
                                 rstd[:, 1, ts].unsqueeze(2).to_broadcast([P, TB, E]), ALU.mult).then_inc(scaled_ok, 1)
                dve.wait_ge(scaled_ok, b + 1)
                dve.wait_ge(shift_ok, 2 * b + 2)
                v_.tensor_tensor(lg[:, ts, :], scaled[:, ts, :], shift[:, ts, :], ALU.add).then_inc(lg_ok, 1)
                if beside is not None:
                    dve.wait_ge(x_in[beside], 16)
                tile_stats(0)
                dve.wait_ge(lg_ok, b + 1)
                for t in range(TB * b, TB * b + TB):
                    last = v_.max(best[:, t, :], lg[:, t, :])
                last.then_inc(best_ok, 1)
                tile_stats(1)
                dve.wait_ge(best_ok, b + 1)
                v_.tensor_tensor(rel[:, ts, :], best[:, ts, :], best[:, ts, 0:1].to_broadcast([P, TB, E]),
                                 ALU.subtract).then_inc(rel_ok, 1)
                for t in range(TB * b, TB * b + TB):
                    last = v_.max_index(bidx[:, t, :], best[:, t, :], lg[:, t, :])
                last.then_inc(idx_ok, 1)
                tile_stats(2)
                dve.wait_ge(idx_ok, b + 1)
                v_.tensor_copy(bidxf[:, ts, :], bidx[:, ts, 0:K]).then_inc(idxf_ok, 1)
                tile_stats(3)
                dve.wait_ge(idxf_ok, b + 1)
                v_.tensor_tensor(oh[:, ts, :, :].rearrange("p t k e -> p (t k) e"),
                                 iota_e[:, :].unsqueeze(1).to_broadcast([P, TB * K, E]),
                                 bidxf[:, ts, :].rearrange("p t k -> p (t k)").unsqueeze(2).to_broadcast([P, TB * K, E]),
                                 ALU.is_equal).then_inc(oh_ok, 1)
                if beside is not None:
                    dve.wait_ge(stat1, 2 * beside + 1)
                    for t in range(TB * beside, TB * beside + TB):
                        last = v_.bn_aggr(mv[:, 0, t, :], stats[:, 0, t, :])
                    last.then_inc(stat1, 1)
                dve.wait_ge(oh_ok, b + 1)
                v_.tensor_tensor(mask[:, ts, :], oh[:, ts, 0, :], oh[:, ts, 1, :], ALU.add).then_inc(mask_ok, 1)
                if beside is not None:
                    add_eps(beside)
                dve.wait_ge(mask_ok, b + 1)
                with nc.allow_low_precision("counts up to 16 are exact in bfloat16"):
                    v_.tensor_reduce(msum[:, b, :], mask[:, ts, :].rearrange("p t e -> p e t"), AX,
                                     ALU.add).then_inc(msum_ok, 1)
                dve.wait_ge(msum_ok, b + 1)
                v_.tensor_tensor(before[:, b + 1, :], before[:, b, :], msum[:, b, :], ALU.add).then_inc(before_ok, 1)

            def weights(b):
                ts = slice(TB * b, TB * b + TB)
                dve.wait_ge(erel_ok, b + 1)
                v_.tensor_reduce(esum[:, ts], erel[:, ts, :], AX, ALU.add).then_inc(esum_ok, 1)
                dve.wait_ge(esum_ok, b + 1)
                v_.reciprocal(einv[:, ts], esum[:, ts]).then_inc(einv_ok, 1)
                dve.wait_ge(einv_ok, b + 1)
                v_.tensor_tensor(zrow[:, ts, :, GATE], erel[:, ts, 0:K],
                                 einv[:, ts].unsqueeze(2).to_broadcast([P, TB, K]), ALU.mult).then_inc(gate_ok, 1)

            def place(b):
                ts = slice(TB * b, TB * b + TB)
                dve.wait_ge(rank_t, b + 1)
                v_.tensor_tensor(slot[:, ts, :], rank_ps[:, ts, :], region[:, :].unsqueeze(1).to_broadcast([P, TB, E]),
                                 ALU.add).then_inc(slot_ok, 1)
                dve.wait_ge(slot_ok, b + 1)
                v_.tensor_tensor(ohslot[:, ts, :, :], oh[:, ts, :, :],
                                 slot[:, ts, :].unsqueeze(2).to_broadcast([P, TB, K, E]), ALU.mult).then_inc(ohslot_ok, 1)
                dve.wait_ge(ohslot_ok, b + 1)
                with nc.allow_low_precision("whole numbers below 2 ** 24, summed in float32"):
                    v_.tensor_reduce(pos[:, ts, :].rearrange("p t k -> p (t k)"),
                                     ohslot[:, ts, :, :].rearrange("p t k e -> p (t k) e"), AX,
                                     ALU.add).then_inc(pos_ok, 1)

            def maxima(b):
                for h in range(2):
                    dve.wait_ge(s_t, 2 * b + h + 1)
                    v_.tensor_reduce(nmax[:, b % 2, 2 * h:2 * h + 2], s_ps[h][:, :, 0:WIN], AX, ALU.max,
                                     negate=True).then_inc(nmax_ok, 1)

            v_.memset(one_row[:, :], 1.0).then_inc(one_ok, 1)
            v_.memset(before[:, 0, :], 0.0)
            v_.memset(ones[:, :], 1.0)
            v_.memset(ones_e[:, :], 1.0)
            v_.memset(h1T[:, :, 0:HALF], 0.0)
            v_.memset(h1T[:, :, HALF + S:PADK], 0.0)
            v_.memset(kT[:, :, 0:HALF], 0.0)
            v_.memset(kT[:, :, HALF + S:PADK], 0.0).then_inc(free_zero, 1)
            norm1_stats(0)
            norm1_apply(0)
            norm2_stats(0)
            dve.wait_ge(wr_in, 16)
            dve.wait_ge(cols_ok, 1)
            v_.tensor_scalar(wg[:, :], wr_sb[:, :], cols[:, GA:GA + 1], None, ALU.mult).then_inc(wg_ok, 1)
            norm1_stats(1)
            dve.wait_ge(sums_t, 1)
            dve.wait_ge(br_in, 16)
            v_.tensor_copy(wg_sum[:, :], sums_ps[:, 0, :])
            v_.tensor_tensor(br_bc[:, :], br_bc[:, :], sums_ps[:, 1, :], ALU.add).then_inc(sums_ok, 1)
            dve.wait_ge(sums_ok, 1)
            dve.wait_ge(routing_consts, 1)
            shift_logits(0)
            choose(0)
            dve.wait_ge(vb_in, 16)
            dve.wait_ge(kqb_t, 1)
            v_.tensor_tensor(vb_bc[:, :], vb_bc[:, :], vb_ps, ALU.add)
            v_.tensor_copy(b2_sum[:, :], b2_ps).then_inc(vb_ok, 1)

            def table_of_blocks():
                steps = [0]

                def after(ins):
                    steps[0] += 1
                    ins.then_inc(table, 1)
                    dve.wait_ge(table, steps[0])

                dve.wait_ge(total_t, 1)
                v_.tensor_copy(count_i[:, :], total_ps[0:1, :]).then_inc(counts_ok, 1)
                after(v_.tensor_tensor(over[:, :, :], total_ps[0:1, :].unsqueeze(2).to_broadcast([1, E, NT]),
                                       iota_128[:, :].unsqueeze(1).to_broadcast([1, E, NT]), ALU.is_gt))
                after(v_.tensor_reduce(nblk[:, :], over[:, :, :], AX, ALU.add))
                after(v_.tensor_tensor_scan(incl[:, :], one_row[:, :], nblk[:, :], 0.0, ALU.mult, ALU.add))
                after(v_.tensor_tensor(past[:, :, :], iota_j[:, :].unsqueeze(2).to_broadcast([1, MAXBLK, E]),
                                       incl[:, :].unsqueeze(1).to_broadcast([1, MAXBLK, E]), ALU.is_ge))
                after(v_.tensor_tensor(pastn[:, :, :], past[:, :, :],
                                       nblk[:, :].unsqueeze(1).to_broadcast([1, MAXBLK, E]), ALU.mult))
                v_.tensor_reduce(eb[:, :], past[:, :, :], AX, ALU.add)
                after(v_.tensor_reduce(excl[:, :], pastn[:, :, :], AX, ALU.add))
                v_.tensor_scalar(expert_i[:, :], eb[:, :], float(E - 1), None, ALU.min)
                after(v_.tensor_tensor(jrel[:, :], iota_j[:, :], excl[:, :], ALU.subtract))
                after(v_.tensor_scalar(startf[:, :], eb[:, :], float(REG), None, ALU.mult))
                after(v_.scalar_tensor_tensor(startf[:, :], jrel[:, :], float(P), startf[:, :], ALU.mult, ALU.add))
                v_.tensor_scalar(start_i[:, :], startf[:, :], float(E * REG), None, ALU.min).then_inc(table_ok, 1)

            def constant_rows():
                dve.wait_ge(c_ok, E // TB)
                v_.tensor_reduce(c_tot[:, :], cw[:, :, :].rearrange("p e h -> p h e"), AX, ALU.add).then_inc(cstep, 1)
                dve.wait_ge(cstep, 1)
                v_.tensor_tensor(c_tot[:, :], c_tot[:, :], b2_sum[:, :], ALU.add).then_inc(cstep, 1)
                dve.wait_ge(cstep, 2)
                v_.tensor_tensor(W1x[:, :, F + FC:WX], c_tot[:, :].unsqueeze(1).to_broadcast([P, E, H]), cw[:, :, :],
                                 ALU.subtract).then_inc(d_ok, 1)

            def probs_turned(b):
                dve.wait_ge(pT_t, b + 1)
                v_.tensor_copy(pTb[:, :, :], pTb_ps[0:CH, :, :]).then_inc(pTb_ok, 1)
                v_.reciprocal(pinv[:, b % 2, :], psums[:, b % 2, :]).then_inc(pinv_ok, 1)

            def attended(b):
                dve.wait_ge(pinv_ok, b + 1)
                dve.wait_ge(pv_t, b + 1)
                v_.tensor_tensor(acc[:, TB * b:TB * b + TB, :], pv_ps,
                                 pinv[:, b % 2, :].unsqueeze(2).to_broadcast([P, TB, H]), ALU.mult).then_inc(acc_ok, 1)

            norm1_apply(1)
            weights(0)
            place(0)
            norm2_stats(1)
            norm1_apply(2)
            norm2_stats(2)
            shift_logits(1)
            choose(1)
            maxima(0)
            for b in range(B):
                if b >= 1:
                    if b + 1 < B:
                        choose(b + 1)
                    if b == 1:
                        constant_rows()
                    probs_turned(b - 1)
                if b + 1 < B:
                    weights(b + 1)
                    place(b + 1)
                if b == 0:
                    norm1_apply(3)
                    norm2_stats(3)
                else:
                    maxima(b)
                    attended(b - 1)
                if b + 2 < B:
                    shift_logits(b + 2)
                if b == B - 2:
                    table_of_blocks()
            def take_w1(j, s, e):
                if not isinstance(j, int) or j >= U:
                    dve.wait_ge(yd_ok, j - U + 1)
                v_.tensor_copy(w1c[:, s, :], W1x[:, bass.ds(e, 1), :].rearrange("p o f -> p (o f)")).then_inc(w1c_ok, 1)

            def relu_part(j, s):
                dve.wait_ge(h_t1, j + 1)
                dve.wait_ge(w1c_ok, j + 1)
                for c in range(FA, FC):
                    last = v_.tensor_scalar(hT[:, s, c, :], h_ps[s][1][:, c - FA, :], w1c[:, s, F + c:F + c + 1], 0.0,
                                            ALU.add, ALU.max)
                last.then_inc(h_dve_ok, 1)

            def take_meta(j, s, value):
                dve.wait_ge(xg_in[s], value)
                v_.tensor_copy(meta_g[:, bass.ds(j, 1)], xg[:, s, GATE:GATE + 1])
                v_.tensor_copy(meta_d[:, bass.ds(j, 1)], xg[:, s, DEST:DEST + 1]).then_inc(meta_ok, 1)

            def add_constant(j, s):
                dve.wait_ge(y_t, j + 1)
                if not isinstance(j, int) or j >= U:
                    dve.wait_ge(y_ok, j - U + 1)
                v_.tensor_tensor(yd[:, s, :], y_ps[:, s, :], w1c[:, s, F + FC:WX], ALU.add).then_inc(yd_ok, 1)

            probs_turned(B - 1)
            dve.wait_ge(W1_in, 16)
            dve.wait_ge(w1b_ok, 1)
            dve.wait_ge(d_ok, 1)
            experts = table_values(expert_i, 0, mybir.EngineType.DVE, E - 1)
            take_w1(0, 0, experts[0])
            take_w1(1, 1, experts[1])
            attended(B - 1)
            take_meta(0, 0, 16)
            take_meta(1, 1, 16)
            relu_part(0, 0)

            def expert_step(j, s, it, ahead2, ahead1, e):
                if ahead2:
                    take_w1(j + 2, (s + 2) % U, e)
                    loads = (s + 2) // U + 1
                    take_meta(j + 2, (s + 2) % U, 16 * loads if it is None else 16 * it + 16 * loads)
                if ahead1:
                    relu_part(j + 1, (s + 1) % U)
                add_constant(j, s)

            experts = table_values(expert_i, 2, mybir.EngineType.DVE, E - 1)
            for s in range(U):
                expert_step(s, s, None, True, True, experts[s])
            with dve.Fori(1, IT - 1) as it:
                experts = table_values(expert_i, U * it + 2, mybir.EngineType.DVE, E - 1)
                for s in range(U):
                    expert_step(U * it + s, s, it, True, True, experts[s])
            experts = table_values(expert_i, MAXBLK - U, mybir.EngineType.DVE, E - 1)
            for s in range(U):
                expert_step(U * (IT - 1) + s, s, IT - 1, s + 2 < U, s + 1 < U, experts[U - 1])

            dve.wait_ge(res_ok, 6 * B)
            for b in range(B):
                ts = slice(TB * b, TB * b + TB)
                dve.wait_ge(yk_in[0][b], 16)
                v_.tensor_tensor(acc[:, ts, :], acc[:, ts, :], yk[:, 0, ts, :], ALU.add).then_inc(sum_ok, 1)
            for ts in OUT_PARTS:
                b = ts.start // TB
                dve.wait_ge(yk_in[1][b], 16)
                dve.wait_ge(sum_ok, b + 1)
                v_.tensor_tensor(acc[:, ts, :], acc[:, ts, :], yk[:, 1, ts, :], ALU.add).then_inc(out_ok, 1)

        @block.scalar
        def _(act):
            a_ = nc.scalar
            act.wait_ge(one_ok, 1)
            a_.activation(warm[:, :], one_row[:, 0:1], ACT.Exp)
            for i, src in enumerate((nm_b1, nm_b2, q_b, k_b, gamma, beta)):
                act.dma_start(rows[NB1 + i:NB1 + i + 1, :], src.unsqueeze(0)).then_inc(rows_in, 16)

            def xn_turned(b):
                act.wait_ge(xT_t, b + 1)
                a_.activation(xnT[:, b % 3, :], xT_ps[b].rearrange("p t c -> p (t c)"), ACT.Copy).then_inc(xnT_ok, 1)

            def normed(b, tiles_done=range(TB)):
                act.wait_ge(nmr_ok, b + 1)
                act.wait_ge(xn_ok, b + 1)
                for t in tiles_done:
                    last = a_.activation(zrow[:, TB * b + t, :, 0:H],
                                         xn[:, TB * b + t, :].unsqueeze(1).to_broadcast([P, K, H]), ACT.Identity,
                                         bias=nmr[:, TB * b + t:TB * b + t + 1],
                                         scale=rstd[:, 1, TB * b + t:TB * b + t + 1])
                if TB - 1 in tiles_done:
                    last.then_inc(z_ok, 1)

            def hidden(b):
                act.wait_ge(h1_t, b + 1)
                a_.activation(h1T[:, b % 2, HALF:HALF + S], h1_ps[:, :], ACT.Relu,
                              bias=cols[:, NB1:NB1 + 1]).then_inc(h1_ok, 1)

            def exps_routing(b):
                act.wait_ge(rel_ok, b + 1)
                a_.activation(erel[:, TB * b:TB * b + TB, :], rel[:, TB * b:TB * b + TB, :], ACT.Exp).then_inc(erel_ok, 1)

            xn_turned(0)
            act.wait_ge(cols_t, 1)
            a_.activation(cols[:, :], cols_ps, ACT.Copy).then_inc(cols_ok, 1)
            act.wait_ge(w2T_t, 1)
            a_.activation(w2T[:, :], w2T_ps, ACT.Copy).then_inc(w2T_ok, 1)
            act.wait_ge(cols_ok, 1)
            a_.activation(rb1[:, :], cols[:, 0:E * FC], ACT.Relu).then_inc(cols_ok, 1)
            act.wait_ge(free_zero, 1)
            hidden(0)
            normed(0, range(TB // 2))
            act.wait_ge(fold_t, 1)
            a_.activation(fold[:, :, :], fold_ps, ACT.Copy).then_inc(fold_ok, 1)
            act.wait_ge(kqb_t, 1)
            a_.activation(kqb[:, 0:1], kqb_ps[:, 0:1], ACT.Identity, bias=cols[:, KB:KB + 1])
            a_.activation(kqb[:, 1:2], kqb_ps[:, 1:2], ACT.Identity, bias=cols[:, QB:QB + 1]).then_inc(kqb_ok, 1)
            act.wait_ge(kqb_ok, 1)
            a_.activation(qbs[:, :], kqb[:, 1:2], ACT.Copy, scale=SCALE).then_inc(kqb_ok, 1)
            act.wait_ge(kqb_ok, 2)

            def exps(b):
                for h in range(2):
                    act.wait_ge(nmax_ok, 2 * b + h + 1)
                    for i in (2 * h, 2 * h + 1):
                        last = a_.activation(prob[:, b % 2, i, :], s_ps[h][:, i % 2, 0:WIN], ACT.Exp,
                                             bias=nmax[:, b % 2, i:i + 1], accum_out=psums[:, b % 2, i:i + 1])
                    last.then_inc(prob_ok, 1)

            def probs_turned(b):
                act.wait_ge(pT_t, b + 1)
                a_.activation(pTa[:, :, :], pTa_ps, ACT.Copy).then_inc(pTa_ok, 1)

            def constant_rows_read(half):
                act.wait_ge(c_t, half + 1)
                a_.activation(cw[:, TB * half:TB * half + TB, :], cw_ps, ACT.Copy).then_inc(c_ok, 1)

            for b in range(B):
                if b >= 2:
                    exps(b - 1)
                if b == 2:
                    normed(3, range(TB // 2))
                if b == 1:
                    act.wait_ge(W1_in, 16)
                    a_.activation(W1x[:, :, F:F + FC], cols[:, 0:E * FC].rearrange("p (e c) -> p e c", c=FC),
                                  ACT.Copy).then_inc(w1b_ok, 1)
                act.wait_ge(k_t, b + 1)
                a_.activation(kT[:, b, HALF:HALF + S], k_ps[:, :], ACT.Identity, bias=kqb[:, 0:1]).then_inc(k_ok, 1)
                if b == 0:
                    exps_routing(0)
                    normed(0, range(TB // 2, TB))
                    xn_turned(1)
                act.wait_ge(v_t, b + 1)
                a_.activation(v[:, b, 0:TB, :], pv_ps, ACT.Copy)
                a_.activation(v[:, b, TB, :], v4_ps, ACT.Copy).then_inc(v_ok, 1)
                act.wait_ge(q_t, b + 1)
                a_.activation(qT[:, b, :], q_ps[:, :], ACT.Identity, bias=qbs[:, 0:1], scale=SCALE).then_inc(q_ok, 1)
                if b == 0:
                    hidden(1)
                    normed(1)
                if b + 1 < B:
                    exps_routing(b + 1)
                if b == 0:
                    constant_rows_read(0)
                if b >= 1:
                    probs_turned(b - 1)
                if b + 2 < B:
                    xn_turned(b + 2)
                if 1 <= b < B - 1:
                    hidden(b + 1)
                if b == 0:
                    exps(0)
                    constant_rows_read(1)
                elif b == 2:
                    normed(3, range(TB // 2, TB))
                elif b + 1 < B:
                    normed(b + 1)
            exps(B - 1)
            probs_turned(B - 1)

            def turn_block(j, s, turned=xgT_ps):
                act.wait_ge(xgT_t, j + 1)
                a_.activation(xgT[:, s, :], turned[:, s, :], ACT.Identity,
                              bias=cols[:, BE:BE + 1], scale=cols[:, GA:GA + 1]).then_inc(xgT_ok, 1)

            def relu_part(j, s):
                act.wait_ge(h_t0, j + 1)
                for c in range(FA):
                    last = a_.activation(hT[:, s, c, :], h_ps[s][0][:, c, :], ACT.Relu, bias=w1c[:, s, F + c:F + c + 1])
                last.then_inc(h_act_ok, 1)

            def weigh(j, s):
                act.wait_ge(yd_ok, j + 1)
                act.wait_ge(meta_ok, j + 1)
                a_.activation(ys[:, bass.ds(j, 1), :].rearrange("p o h -> p (o h)"), yd[:, s, :], ACT.Copy,
                              scale=meta_g[:, bass.ds(j, 1)]).then_inc(y_ok, 1)

            turn_block(0, 0, xgT0_ps)
            turn_block(1, 1)
            relu_part(0, 0)

            def expert_step(j, s, ahead2, ahead1, behind1):
                if ahead2:
                    turn_block(j + 2, (s + 2) % U)
                if ahead1:
                    relu_part(j + 1, (s + 1) % U)
                if behind1:
                    weigh(j - 1, (s - 1) % U)

            for s in range(U):
                expert_step(s, s, True, True, s >= 1)
            with act.Fori(1, IT - 1) as it:
                for s in range(U):
                    expert_step(U * it + s, s, True, True, True)
            for s in range(U):
                expert_step(U * (IT - 1) + s, s, s + 2 < U, s + 1 < U, True)
            weigh(MAXBLK - 1, U - 1)

            act.wait_ge(y_out, 16 * MAXBLK)
            for k in range(K):
                for b in range(1, B, 2):
                    ts = slice(TB * b, TB * b + TB)
                    act.dma_start(yk[:, k, ts, :], yt[:, k, ts, :]).then_inc(yk_in[k][b], 16)

        @block.tensor
        def _(pe):
            t_ = nc.tensor

            def turn_xn(b):
                pe.wait_ge(xn_ok, b + 1)
                for i in range(TB):
                    last = t_.transpose(xT_ps[b][:, i, :], xn[:, TB * b + i, :], ident[:, :])
                last.then_inc(xT_t, 1)

            def hidden(b):
                pe.wait_ge(xnT_ok, b + 1)
                if b >= 1:
                    pe.wait_ge(k_ok, b)
                t_.matmul(h1_ps[:, :], w1_sb[:, :], xnT[:, b % 3, :], start=True, stop=True).then_inc(h1_t, 1)

            def logits(b):
                pe.wait_ge(xnT_ok, b + 1)
                if b >= 1:
                    pe.wait_ge(slot_ok, b)
                for i in range(TB):
                    last = t_.matmul(logit_ps[:, TB * b + i, :], xnT[:, b % 3, i * P:(i + 1) * P], wg[:, :],
                                     start=True, stop=True)
                last.then_inc(logit_t, 1)

            pe.wait_ge(free_zero, 1)
            for _ in range(WARMUP):
                t_.matmul(bank[4][:, 0:P], ones[:, :], ones[:, :], start=True, stop=True)
            pe.wait_ge(ident_ok, 1)
            turn_xn(0)
            pe.wait_ge(rows_in, 16 * 6)
            pe.wait_ge(b_in, 16 * 2)
            t_.transpose(cols_ps, rows[:, :], ident[0:NROWS, 0:NROWS]).then_inc(cols_t, 1)
            pe.wait_ge(w2_in, 16)
            t_.transpose(w2T_ps, w2_sb[:, :], ident[:, :]).then_inc(w2T_t, 1)
            pe.wait_ge(cols_ok, 1)
            pe.wait_ge(wr_in, 16)
            for i, c in enumerate((GA, BE)):
                last = t_.matmul(sums_ps[:, i, :], cols[:, c:c + 1].to_broadcast([H, P]), wr_sb[:, :],
                                 start=True, stop=True)
            last.then_inc(sums_t, 1)
            pe.wait_ge(w1_in, 16)
            hidden(0)
            pe.wait_ge(wg_ok, 1)
            logits(0)
            pe.wait_ge(w2T_ok, 1)
            pe.wait_ge(wa_in, 48)
            t_.matmul(fold_ps, w2T[:, :], wkqv[:, :, :], start=True, stop=True).then_inc(fold_t, 1)
            pe.wait_ge(cols_ok, 2)
            for i in range(2):
                t_.matmul(kqb_ps[:, i:i + 1], wkqv[:, i, :], cols[:, NB2:NB2 + 1], start=True, stop=True)
            t_.matmul(vb_ps, cols[:, NB2:NB2 + 1].to_broadcast([H, P]), wkqv[:, 2, :],
                      start=True, stop=True)
            t_.matmul(b2_ps, ones_e[B2:B2 + E, :], rows[B2:B2 + E, :], start=True, stop=True).then_inc(kqb_t, 1)

            def constant_row(e):
                for c in range(FC):
                    last = t_.matmul(cw_ps[:, e % TB, :], rb1[:, e * FC + c:e * FC + c + 1].to_broadcast([P, P]),
                                     W2s[:, e, c, :], start=(c == 0), stop=(c == FC - 1))
                if e % TB == TB - 1:
                    last.then_inc(c_t, 1)

            def scores(b):
                pe.wait_ge(q_ok, b + 1)
                for h in range(2):
                    if b >= 1:
                        pe.wait_ge(prob_ok, 2 * b - 1 + h)
                    for i in (2 * h, 2 * h + 1):
                        t_.matmul(s_ps[h][:, i % 2, 0:WIN], qT[:, b, i * P:(i + 1) * P],
                                  kT[:, b, i * P:i * P + WIN], start=True, stop=False)
                        last = t_.matmul(s_ps[h][:, i % 2, 0:WIN], identb[:, :], band[:, i, :], start=False, stop=True)
                    last.then_inc(s_t, 1)

            def turn_probs(b):
                pe.wait_ge(prob_ok, 2 * b + 2)
                if b >= 1:
                    pe.wait_ge(pTa_ok, b)
                    pe.wait_ge(pTb_ok, b)
                else:
                    pe.wait_ge(c_ok, E // TB)
                for i in range(TB):
                    t_.transpose(pTa_ps[:, i, :], prob[:, b % 2, i, 0:P], ident[:, :])
                    last = t_.transpose(pTb_ps[0:CH, i, :], prob[:, b % 2, i, P:WIN], ident[:, :])
                last.then_inc(pT_t, 1)

            def attend(b):
                pe.wait_ge(pTa_ok, b + 1)
                pe.wait_ge(pTb_ok, b + 1)
                for i in range(TB):
                    t_.matmul(pv_ps[:, i, :], pTa[:, i, :], v[:, b, i, :], start=True, stop=False)
                    last = t_.matmul(pv_ps[:, i, :], pTb[:, i, :], v[0:CH, b, i + 1, :], start=False, stop=True)
                last.then_inc(pv_t, 1)

            def ranks(b):
                pe.wait_ge(mask_ok, b + 1)
                r = rank_ps[:, TB * b:TB * b + TB, :]
                t_.matmul(r, upper[:, :], mask[:, TB * b:TB * b + TB, :], start=True, stop=False, skip_group_check=True)
                for i in range(TB - 1):
                    t_.matmul(rank_ps[:, TB * b + i + 1:TB * b + TB, :], ones[:, :],
                              mask[:, TB * b + i:TB * b + i + 1, :].to_broadcast([P, TB - 1 - i, E]),
                              start=False, stop=False, skip_group_check=True)
                if b >= 1:
                    pe.wait_ge(before_ok, b)
                t_.matmul(r, ones[:, :], before[:, b:b + 1, :].to_broadcast([P, TB, E]),
                          start=False, stop=True, skip_group_check=True).then_inc(rank_t, 1)

            for b in range(B):
                pe.wait_ge(h1_ok, b + 1)
                if b == 0:
                    pe.wait_ge(fold_ok, 1)
                t_.matmul(k_ps[:, :], fold[:, 0, :], h1T[:, b % 2, HALF:HALF + S],
                          start=True, stop=True).then_inc(k_t, 1)
                if b == 0:
                    pe.wait_ge(routing_consts, 1)
                    ranks(0)
                if b >= 2:
                    pe.wait_ge(acc_ok, b - 1)
                    pe.wait_ge(pTb_ok, b - 1)
                for i in range(TB + 1):
                    if b == 0 and i == TB:
                        pe.wait_ge(vb_ok, 1)
                    last = t_.matmul(pv_ps[:, i, :] if i < TB else v4_ps, h1T[:, b % 2, i * P:(i + 1) * P],
                                     fold[:, 2, :], start=True, stop=True)
                last.then_inc(v_t, 1)
                if b == 0:
                    turn_xn(1)
                    pe.wait_ge(xnT_ok, 1)
                elif b + 1 < B:
                    pe.wait_ge(xnT_ok, b + 2)
                t_.matmul(q_ps[:, :], fold[:, 1, :], h1T[:, b % 2, HALF:HALF + S],
                          start=True, stop=True).then_inc(q_t, 1)
                if b == 0:
                    hidden(1)
                    logits(1)
                    pe.wait_ge(consts, 1)
                    scores(0)
                    pe.wait_ge(W2_in, 16)
                    for e in range(TB):
                        constant_row(e)
                    ranks(1)
                    pe.wait_ge(q_ok, 1)
                    turn_xn(2)
                else:
                    pe.wait_ge(v_ok, b + 1)
                    turn_probs(b - 1)
                if b >= 1:
                    if b + 1 < B:
                        ranks(b + 1)
                    if b + 2 < B:
                        pe.wait_ge(q_ok, b + 1)
                        turn_xn(b + 2)
                    if b + 1 < B:
                        hidden(b + 1)
                    scores(b)
                    attend(b - 1)
                if b == 0:
                    pe.wait_ge(c_ok, 1)
                    for e in range(TB, 2 * TB):
                        constant_row(e)
                if b + 2 < B:
                    logits(b + 2)
                if b == B - 2:
                    pe.wait_ge(before_ok, B)
                    pe.wait_ge(slot_ok, B)
                    t_.matmul(total_ps, ones[:, :], before[:, B, :], start=True, stop=True).then_inc(total_t, 1)

            turn_probs(B - 1)
            pe.wait_ge(acc_ok, B - 1)
            attend(B - 1)

            def turn_block(j, s, value, turned=xgT_ps):
                pe.wait_ge(xg_in[s], value)
                if not isinstance(j, int) or j >= 2:
                    pe.wait_ge(xgT_ok, j)
                t_.transpose(turned[:, s, :], xg[:, s, 0:H], ident[:, :]).then_inc(xgT_t, 1)

            def first(j, s, turned):
                if not turned:
                    pe.wait_ge(xgT_ok, j + 1)
                pe.wait_ge(w1c_ok, j + 1)
                for half, done in enumerate((h_t0, h_t1)):
                    for f in range(FA * half, FC if half else FA):
                        last = t_.matmul(h_ps[s][half][:, f - FA * half, :], w1c[:, s, f * P:(f + 1) * P], xgT[:, s, :],
                                         start=True, stop=True)
                    last.then_inc(done, 1)

            def second(j, s, e):
                pe.wait_ge(h_act_ok, j + 1)
                pe.wait_ge(h_dve_ok, j + 1)
                if not isinstance(j, int) or j >= 1:
                    pe.wait_ge(yd_ok, j)
                for c in range(FC):
                    last = t_.matmul(y_ps[:, s, :], hT[:, s, c, :],
                                     W2s[:, bass.ds(e, 1), c, :].rearrange("p o h -> p (o h)"),
                                     start=(c == 0), stop=(c == FC - 1))
                last.then_inc(y_t, 1)

            pe.wait_ge(table_ok, 1)
            turn_block(0, 0, 16, xgT0_ps)
            turn_block(1, 1, 16)
            first(0, 0, False)
            pe.wait_ge(acc_ok, B)
            pe.wait_ge(c_ok, E // TB)

            def ahead(it, s, ahead2, ahead1):
                j = U * it + s
                if ahead2:
                    turn_block(j + 2, (s + 2) % U, 16 * it + 16 * ((s + 2) // U) + 16)
                if ahead1:
                    first(j + 1, (s + 1) % U, ahead2)

            def expert_steps(it, last):
                ahead(it, 0, True, True)
                experts = table_values(expert_i, U * it, mybir.EngineType.PE, E - 1)
                second(U * it, 0, experts[0])
                for s in range(1, U):
                    ahead(it, s, s + 2 < U or not last, s + 1 < U or not last)
                    second(U * it + s, s, experts[s])

            with pe.Fori(0, IT - 1) as it:
                expert_steps(it, False)
            expert_steps(IT - 1, True)


_INS = ['L0_attn_x', 'L0_attn_nm_w1', 'L0_attn_nm_b1', 'L0_attn_nm_w2', 'L0_attn_nm_b2', 'L0_attn_q_w',
        'L0_attn_q_b', 'L0_attn_k_w', 'L0_attn_k_b', 'L0_attn_v_w', 'L0_attn_v_b', 'L0_ffn_gamma', 'L0_ffn_beta',
        'L0_ffn_Wr', 'L0_ffn_br', 'L0_ffn_W1', 'L0_ffn_b1', 'L0_ffn_W2', 'L0_ffn_b2']
_OUTS = [((4, 512, 128), 'float32')]


def kernel(**inputs):
    import numpy as _np
    import concourse.bacc as _bacc
    from concourse import mybir as _mybir
    from concourse.bass_utils import run_bass_kernel_spmd as _run

    nc = _bacc.Bacc("TRN2", target_bir_lowering=False, num_devices=1)
    arrays, args = {}, []
    for name in _INS:
        a = _np.ascontiguousarray(inputs[name])
        arrays[f"in_{name}_dram"] = a
        args.append(nc.dram_tensor(f"in_{name}_dram", a.shape, _mybir.dt.from_np(a.dtype), kind="ExternalInput").ap())
    for i, (shape, dtype) in enumerate(_OUTS):
        dt = _mybir.dt.from_np(_np.dtype(dtype))
        args.append(nc.dram_tensor(f"out_{i}_dram", shape, dt, kind="ExternalOutput").ap())
    build(nc, *args)
    r = _run(nc, [arrays], core_ids=[0])
    return r.results[0]["out_0_dram"]
```
